# Optimizing a Trainium2 kernel written in Bass

```python
import numpy as np
import jax
import jax.numpy as jnp

def _softmax(x, axis=-1):
    return jax.nn.softmax(x, axis=axis)

def _gelu(x):
    return jax.nn.gelu(x, approximate=True)

def _silu(x):
    return jax.nn.silu(x)

def _sigmoid(x):
    return jax.nn.sigmoid(x)

def _layernorm(x, axis=-1, eps=1e-05):
    m = jnp.mean(x, axis=axis, keepdims=True)
    v = jnp.var(x, axis=axis, keepdims=True)
    return (x - m) / jnp.sqrt(v + eps)

def _scatter_add(tgt, idx, src, axis=0):
    return tgt.at[idx].add(src)

def _segment_sum(src, seg, n):
    return jax.ops.segment_sum(src, seg, n)
kernel_name = 'mk_seq_postln_d2_jaxref_r8_617405'

def setup_inputs(seed: int=0):
    np.random.seed(seed)
    _w = jnp.asarray

    def _L0_attn_setup():
        import jax, jax.numpy as jnp
        import numpy as np
        B, S, D = (2, 256, 256)
        HQ, HKV = (32, 8)
        DH = D // HQ
        NUM_REP = HQ // HKV
        key = jax.random.key(seed)
        k1, k2, k3, k4, k5 = jax.random.split(key, 5)
        scale = 0.02
        return {'x': jax.random.normal(k1, (B, S, D), dtype=jnp.float32), 'Wq': jax.random.normal(k2, (D, HQ * DH), dtype=jnp.float32) * scale, 'Wk': jax.random.normal(k3, (D, HKV * DH), dtype=jnp.float32) * scale, 'Wv': jax.random.normal(k4, (D, HKV * DH), dtype=jnp.float32) * scale, 'Wo': jax.random.normal(k5, (HQ * DH, D), dtype=jnp.float32) * scale}
    _L0_attn_in = _L0_attn_setup()

    def _L0_ffn_setup():
        import jax, jax.numpy as jnp
        import numpy as np
        B, S, H, I = (1, 64, 256, 768)

        def _quantized_matmul(x, w, scale):
            wq = w.astype(jnp.float8_e4m3fn).astype(x.dtype)
            y = jnp.einsum('bsi,io->bso', x, wq)
            return y * scale
        key = jax.random.key(seed)
        ks = jax.random.split(key, 7)
        return {'x': jax.random.normal(ks[0], (B, S, H), dtype=jnp.float32), 'gate_w': jax.random.normal(ks[1], (H, I), dtype=jnp.float32) * 0.02, 'up_w': jax.random.normal(ks[2], (H, I), dtype=jnp.float32) * 0.02, 'down_w': jax.random.normal(ks[3], (I, H), dtype=jnp.float32) * 0.02, 'gate_scale': jax.random.uniform(ks[4], (I,), dtype=jnp.float32, minval=0.5, maxval=1.5), 'up_scale': jax.random.uniform(ks[5], (I,), dtype=jnp.float32, minval=0.5, maxval=1.5), 'down_scale': jax.random.uniform(ks[6], (H,), dtype=jnp.float32, minval=0.5, maxval=1.5)}
    _L0_ffn_in = _L0_ffn_setup()

    def _L1_attn_setup():
        import jax, jax.numpy as jnp
        import numpy as np
        HIDDEN = 256
        N_HEADS = 16
        N_KV = 8
        HEAD_DIM = HIDDEN // N_HEADS
        GROUPS = N_HEADS // N_KV
        N_LAYERS = 28
        key = jax.random.key(seed)
        k0, k1, k2, k3, k4 = jax.random.split(key, 5)
        std = HIDDEN ** (-0.5)
        o_std = (2 * N_LAYERS) ** (-0.5)
        hidden_states = jax.random.normal(k0, (1, 256, HIDDEN), dtype=jnp.float32)
        wq = jax.random.normal(k1, (N_HEADS * HEAD_DIM, HIDDEN), dtype=jnp.float32) * std
        wk = jax.random.normal(k2, (N_KV * HEAD_DIM, HIDDEN), dtype=jnp.float32) * std
        wv = jax.random.normal(k3, (N_KV * HEAD_DIM, HIDDEN), dtype=jnp.float32) * std
        wo = jax.random.normal(k4, (HIDDEN, HIDDEN), dtype=jnp.float32) * o_std
        return {'hidden_states': hidden_states, 'wq': wq, 'wk': wk, 'wv': wv, 'wo': wo}
    _L1_attn_in = _L1_attn_setup()

    def _L1_ffn_setup():
        import jax, jax.numpy as jnp
        import numpy as np
        HIDDEN = 256
        INTER = 688
        LUT_SIZE = 16

        def _ghost_linear(x, idx, lut):
            w = lut[idx]
            return jnp.einsum('bsh,oh->bso', x, w)
        key = jax.random.key(seed)
        k_x, k_lut, k_g, k_u, k_d = jax.random.split(key, 5)
        x = jax.random.normal(k_x, (2, 512, HIDDEN), dtype=jnp.float32)
        lut = jax.random.normal(k_lut, (LUT_SIZE,), dtype=jnp.float32) * 0.02
        gate_idx = jax.random.randint(k_g, (INTER, HIDDEN), 0, LUT_SIZE, dtype=jnp.int32)
        up_idx = jax.random.randint(k_u, (INTER, HIDDEN), 0, LUT_SIZE, dtype=jnp.int32)
        down_idx = jax.random.randint(k_d, (HIDDEN, INTER), 0, LUT_SIZE, dtype=jnp.int32)
        return {'x': x, 'lut': lut, 'gate_idx': gate_idx, 'up_idx': up_idx, 'down_idx': down_idx}
    _L1_ffn_in = _L1_ffn_setup()
    _d = {'L0_attn_x': _L0_attn_in['x'], 'L0_attn_Wq': _L0_attn_in['Wq'], 'L0_attn_Wk': _L0_attn_in['Wk'], 'L0_attn_Wv': _L0_attn_in['Wv'], 'L0_attn_Wo': _L0_attn_in['Wo'], 'L0_ffn_gate_w': _L0_ffn_in['gate_w'], 'L0_ffn_up_w': _L0_ffn_in['up_w'], 'L0_ffn_down_w': _L0_ffn_in['down_w'], 'L0_ffn_gate_scale': _L0_ffn_in['gate_scale'], 'L0_ffn_up_scale': _L0_ffn_in['up_scale'], 'L0_ffn_down_scale': _L0_ffn_in['down_scale'], 'L1_attn_wq': _L1_attn_in['wq'], 'L1_attn_wk': _L1_attn_in['wk'], 'L1_attn_wv': _L1_attn_in['wv'], 'L1_attn_wo': _L1_attn_in['wo'], 'L1_ffn_lut': _L1_ffn_in['lut'], 'L1_ffn_gate_idx': _L1_ffn_in['gate_idx'], 'L1_ffn_up_idx': _L1_ffn_in['up_idx'], 'L1_ffn_down_idx': _L1_ffn_in['down_idx']}
    _x0 = _d['L0_attn_x']
    _d['L0_attn_x'] = jax.random.normal(jax.random.fold_in(jax.random.key(seed), 1), (4, 256, 256), dtype=_x0.dtype)
    del _x0
    return _d

def reference(L0_attn_x, L0_attn_Wq, L0_attn_Wk, L0_attn_Wv, L0_attn_Wo, L0_ffn_gate_w, L0_ffn_up_w, L0_ffn_down_w, L0_ffn_gate_scale, L0_ffn_up_scale, L0_ffn_down_scale, L1_attn_wq, L1_attn_wk, L1_attn_wv, L1_attn_wo, L1_ffn_lut, L1_ffn_gate_idx, L1_ffn_up_idx, L1_ffn_down_idx):

    def _L0_attn_ref(x, Wq, Wk, Wv, Wo):
        import jax, jax.numpy as jnp
        import numpy as np
        B, S, D = (2, 256, 256)
        HQ, HKV = (32, 8)
        DH = D // HQ
        NUM_REP = HQ // HKV
        b, s, _ = x.shape
        xq = (x @ Wq).reshape(b, s, HQ, DH)
        xk = (x @ Wk).reshape(b, s, HKV, DH)
        xv = (x @ Wv).reshape(b, s, HKV, DH)
        keys = jnp.repeat(xk, NUM_REP, axis=2)
        values = jnp.repeat(xv, NUM_REP, axis=2)
        scores = jnp.einsum('bqhd,bkhd->bhqk', xq, keys) / jnp.sqrt(jnp.float32(DH))
        probs = jax.nn.softmax(scores.astype(jnp.float32), axis=-1).astype(xq.dtype)
        context = jnp.einsum('bhqk,bkhd->bqhd', probs, values)
        context = context.reshape(b, s, HQ * DH)
        return context @ Wo

    def _L0_ffn_ref(x, gate_w, up_w, down_w, gate_scale, up_scale, down_scale):
        import jax, jax.numpy as jnp
        import numpy as np
        B, S, H, I = (1, 64, 256, 768)

        def _quantized_matmul(x, w, scale):
            wq = w.astype(jnp.float8_e4m3fn).astype(x.dtype)
            y = jnp.einsum('bsi,io->bso', x, wq)
            return y * scale
        gate = jax.nn.silu(_quantized_matmul(x, gate_w, gate_scale))
        up = _quantized_matmul(x, up_w, up_scale)
        fuse = gate * up
        return _quantized_matmul(fuse, down_w, down_scale)

    def _L1_attn_ref(hidden_states, wq, wk, wv, wo):
        import jax, jax.numpy as jnp
        import numpy as np
        HIDDEN = 256
        N_HEADS = 16
        N_KV = 8
        HEAD_DIM = HIDDEN // N_HEADS
        GROUPS = N_HEADS // N_KV
        N_LAYERS = 28
        b, s, _ = hidden_states.shape
        q = hidden_states @ wq.T
        k = hidden_states @ wk.T
        v = hidden_states @ wv.T
        q = q.reshape(b, s, N_HEADS, HEAD_DIM).transpose(0, 2, 1, 3)
        k = k.reshape(b, s, N_KV, HEAD_DIM).transpose(0, 2, 1, 3)
        v = v.reshape(b, s, N_KV, HEAD_DIM).transpose(0, 2, 1, 3)
        k = jnp.repeat(k, GROUPS, axis=1)
        v = jnp.repeat(v, GROUPS, axis=1)
        scale = 1.0 / jnp.sqrt(jnp.float32(HEAD_DIM))
        attn = jnp.einsum('bhqd,bhkd->bhqk', q, k) * scale
        attn = jax.nn.softmax(attn.astype(jnp.float32), axis=-1).astype(q.dtype)
        out = jnp.einsum('bhqk,bhkd->bhqd', attn, v)
        out = out.transpose(0, 2, 1, 3).reshape(b, s, HIDDEN)
        return out @ wo.T

    def _L1_ffn_ref(x, lut, gate_idx, up_idx, down_idx):
        import jax, jax.numpy as jnp
        import numpy as np
        HIDDEN = 256
        INTER = 688
        LUT_SIZE = 16

        def _ghost_linear(x, idx, lut):
            w = lut[idx]
            return jnp.einsum('bsh,oh->bso', x, w)
        gate = _ghost_linear(x, gate_idx, lut)
        up = _ghost_linear(x, up_idx, lut)
        h = jax.nn.silu(gate) * up
        return _ghost_linear(h, down_idx, lut)
    x = L0_attn_x
    x = _layernorm(x + _L0_attn_ref(x, L0_attn_Wq, L0_attn_Wk, L0_attn_Wv, L0_attn_Wo), axis=-1)
    x = _layernorm(x + _L0_ffn_ref(x, L0_ffn_gate_w, L0_ffn_up_w, L0_ffn_down_w, L0_ffn_gate_scale, L0_ffn_up_scale, L0_ffn_down_scale), axis=-1)
    x = _layernorm(x + _L1_attn_ref(x, L1_attn_wq, L1_attn_wk, L1_attn_wv, L1_attn_wo), axis=-1)
    x = _layernorm(x + _L1_ffn_ref(x, L1_ffn_lut, L1_ffn_gate_idx, L1_ffn_up_idx, L1_ffn_down_idx), axis=-1)
    return x

_drawn_inputs = setup_inputs


def setup_inputs(seed=0):
    import zlib

    import numpy as np

    out = dict(_drawn_inputs(seed))
    spreads = {}
    factors = {'L0_attn_Wq': 8.0,
     'L0_attn_Wk': 8.0,
     'L0_attn_Wv': 4.031,
     'L0_attn_Wo': 4.009,
     'L0_ffn_gate_scale': 4.822,
     'L0_ffn_up_scale': 5.612,
     'L0_ffn_down_scale': 5.469}
    for name, (base, spread) in spreads.items():
        noise = np.random.default_rng([zlib.crc32(name.encode()), seed]).standard_normal(out[name].shape)
        drawn = base * np.exp(spread * noise) if base else spread * noise
        out[name] = jnp.asarray(drawn.astype(out[name].dtype))
    for name, factor in factors.items():
        out[name] = (out[name] * factor).astype(out[name].dtype)
    return out
```

```python
from contextlib import ExitStack

import concourse.bass as bass
from concourse import mybir

P = 128
F32 = mybir.dt.float32
BF16 = mybir.dt.bfloat16
FP8 = mybir.dt.float8e4
I32 = mybir.dt.int32
ALU = mybir.AluOpType
ACT = mybir.ActivationFunctionType
AX = mybir.AxisListType

B, S, D = 4, 256, 256
HEADS = (32, 16)
KV = (8, 8)
I0, I1 = 768, 688
LUT = 16
EPS = 1e-5
DH = tuple(D // h for h in HEADS)
UNITS = tuple(h * 2 * S // 1024 for h in HEADS)
JOBS = 2 * B
DT = D // P
TT = S // P

Q_PART = (0, 0, 0, 1, 1, 2)
K_PART = (0, 1, 2, 0, 1, 0)
NPROD = len(Q_PART)
STACK = tuple(NPROD * d for d in DH)

PB_UNITS = 6
NST = 3
Q8_W = 768
LUT_W = 268
W1_COLS = 2 * DT * I1 + 6 * D
N_Q8 = (2 * DT * I0 + 6 * D) // Q8_W
N_LUT = W1_COLS // LUT_W


def layer(j):
    return j // B


def unit0(j):
    return sum(UNITS[layer(i)] for i in range(j))


def plan():
    at = []
    for j in range(JOBS):
        n = UNITS[layer(j)]
        for u in range(n):
            at.append((j + (u + 0.5) / n, ("score", j, u)))
            at.append((j - 1 + 0.72 * (u + 0.6) / n, ("max", j, u)))
        at.append((j - 0.24, ("mt", j)))
        for r in range(4):
            at.append((j + (r + 1) / 4 + 1.2 / n, ("pv", j, r)))
        for p in range(2):
            t = j + (p + 1) / 2 + 1.3 / n
            at.append((t, ("bounce", j, p)))
            at.append((t + 0.15, ("recip", j, p)))
            at.append((t + 0.30, ("norm", j, p)))
        t = j + 1.31 + 1.5 / n
        at.append((t, ("wo", j)))
        at.append((t + 0.10, ("tr", j, 0)))
        for i in range(6):
            at.append((t + 0.13 + 0.05 * i, ("gu", j, i)))
        at.append((j + 1.95, ("down", j)))
        if layer(j) == 0:
            at.append((j + 2.04, ("tr", j, 1)))
            start = j + 2.08
            at.append((start, ("q", j + B)))
            at.append((start + 0.05, ("kv", j + B)))
        else:
            at.append((j + 2.04, ("out", j)))
        if j < B:
            start = -2 if j == 0 else j - 1.9
            at.append((start, ("q", j)))
            at.append((start + 0.05, ("kv", j)))
    for c in range(N_Q8):
        at.append((-0.7 + 0.2 * c, ("q8", c)))
    for c in range(N_LUT):
        at.append((1.0 + 0.2 * c, ("lutmask", c)))
        at.append((1.1 + 0.2 * c, ("lutpick", c)))
    return [step for _, step in sorted(at, key=lambda x: x[0])]


def two_layer_kernel(nc, x, xt, wq0, wk0, wv0, wo0, gate0, up0, down0, gs0, us0, ds0,
                     wq1, wk1, wv1, wo1, lut, gidx, uidx, didx, out):
    steps = plan()
    FILL = ("q", "kv", "mt", "wo", "tr", "gu", "down")
    fill = {}
    norms = {}
    trs = {}
    for step in steps:
        if step[0] in FILL:
            fill[step] = len(fill)
        if step[0] in ("wo", "down"):
            norms[step] = len(norms)
        if step[0] == "tr":
            trs[step] = len(trs)

    with ExitStack() as ctx:
        def sb(name, shape, dt=F32):
            return ctx.enter_context(nc.sbuf_tensor(name, shape, dt))

        def pb(name, shape, dt=F32):
            return ctx.enter_context(nc.psum_tensor(name, shape, dt))

        def sem(name):
            return ctx.enter_context(nc.semaphore(name))

        X = sb("X", [P, B, TT, D])
        XT = sb("XT", [P, B, DT, S])
        PB = sb("PB", [P, PB_UNITS, 2, 2, S])
        QS = sb("QS", [P, NST, 16, S], BF16)
        KS0 = sb("KS0", [P, NST, 4, S], BF16)
        KS1 = sb("KS1", [P, NST, 8, S], BF16)
        VP0 = sb("VP0", [P, NST, 2, 8, 48])
        VP1 = sb("VP1", [P, NST, 2, 8, 32])
        QP = sb("QP", [P, 3, 2 * S], BF16)
        QR = sb("QR", [P, 2 * S])
        KP = sb("KP", [P, 3, S], BF16)
        KR = sb("KR", [P, S])
        MX = sb("MX", [P, 2, TT, 32])
        MP = sb("MP", [32, 2, S], BF16)
        ST = sb("ST", [P, 2, 2 * S])
        SUMS = sb("SUMS", [P, 2, 32])
        RCP = sb("RCP", [P, 2, 32])
        OP = sb("OP", [P, 2, 2, S])
        OR = sb("OR", [P, 2, 2, S])
        ON = sb("ON", [P, 2, 2, S])
        WQ = [sb("WQ0", [P, DT, D]), sb("WQ1", [P, DT, D])]
        WK = [sb("WK0", [P, DT, 64]), sb("WK1", [P, DT, 128])]
        WV = [sb("WV0", [P, DT, 64]), sb("WV1", [P, DT, 128])]
        WO = [sb("WO0", [P, 2, D]), sb("WO1", [P, 2, D])]
        HT = sb("HT", [P, 6, S])
        TH = sb("TH", [P, 2, S])
        AA = sb("AA", [P, S])
        W0 = sb("W0", [P, N_Q8 * Q8_W])
        W1 = sb("W1", [P, W1_COLS], I32)
        DS = sb("DS", [P, D])
        YD = sb("YD", [P, TT, D])
        RAW = sb("RAW", [P, Q8_W])
        Q8A = sb("Q8A", [P, Q8_W], FP8)
        Q8B = sb("Q8B", [P, Q8_W], FP8)
        BIG = sb("BIG", [P, Q8_W], I32)
        QB = sb("QB", [P, Q8_W])
        LB = sb("LB", [P, 4, LUT_W], I32)
        LB0 = sb("LB0", [P, LUT_W])
        LV = sb("LV", [P, 8, LUT_W])
        LT = sb("LT", [P, LUT])
        LD = sb("LD", [P, LUT // 2])
        GS = sb("GS", [P, 6])
        US = sb("US", [P, 6])
        GSH = sb("GSH", [P, 6])
        GUS = sb("GUS", [P, 6])
        IDN = sb("IDN", [P, P])
        BST = sb("BST", [P, TT, 6])
        MV = sb("MV", [P, TT, 2])
        RSTD = sb("RSTD", [P, TT])
        VE = sb("VE", [P, TT])
        NMR = sb("NMR", [P, TT])
        NHALF = sb("NHALF", [P, TT])

        SC = [pb(f"SC{i}", [P, 2, S]) for i in range(3)]
        MM = [pb(f"MM{i}", [P, 2, S]) for i in range(2)]
        PV = pb("PV", [P, 2, S])
        FB = [pb(f"FB{i}", [P, 2 * S]) for i in range(2)]

        dq = nc.dram_tensor("dq", (JOBS, 3, D, S), BF16, kind="Internal").ap()
        dk = nc.dram_tensor("dk", (JOBS, 3, P, S), BF16, kind="Internal").ap()
        do = nc.dram_tensor("do", (JOBS, 2, P, 2 * S), F32, kind="Internal").ap()
        dr = nc.dram_tensor("dr", (JOBS, 2, 4096), F32, kind="Internal").ap()

        ld_x = sem("ld_x")
        ld_x0 = sem("ld_x0")
        ld_w0 = sem("ld_w0")
        ld_w1 = sem("ld_w1")
        ld_s = sem("ld_s")
        ld_raw = sem("ld_raw")
        ld_idx = sem("ld_idx")
        idn_zero = sem("idn_zero")
        const_pool = sem("const_pool")
        ones_dve = sem("ones_dve")
        scales_dve = sem("scales_dve")
        fill_ready = sem("fill_ready")
        fill_free = [sem(f"fill_free{i}") for i in range(2)]
        q_hi = sem("q_hi")
        k_hi = sem("k_hi")
        q_parts = sem("q_parts")
        k_parts = sem("k_parts")
        dq_wr = sem("dq_wr")
        dk_wr = sem("dk_wr")
        stack_in = [sem(f"stack_in{i}") for i in range(NST)]
        max_mm = sem("max_mm")
        max_red = sem("max_red")
        m_hi = sem("m_hi")
        m_parts = sem("m_parts")
        m_rows = sem("m_rows")
        score_mm = sem("score_mm")
        exp_done = sem("exp_done")
        pv_mm = sem("pv_mm")
        staged = sem("staged")
        do_wr = sem("do_wr")
        sums_in = sem("sums_in")
        recip_done = sem("recip_done")
        dr_wr = sem("dr_wr")
        o_in = [sem(f"o_in{i}") for i in range(2)]
        normed = sem("normed")
        mv_done = sem("mv_done")
        x_new = sem("x_new")
        xt_new = sem("xt_new")
        th_done = sem("th_done")
        q8_cast = sem("q8_cast")
        q8_used = sem("q8_used")
        bit_done = sem("bit_done")
        level1 = sem("level1")
        lut_done = sem("lut_done")
        out_wr = sem("out_wr")
        dve_own = sem("dve_own")
        pool_own = sem("pool_own")
        act_own = sem("act_own")

        block = ctx.enter_context(nc.Block())

        def wait_free(eng, n):
            eng.wait_ge(fill_free[n % 2], n // 2 + 1)

        def stack_count(j):
            return 16 * sum(24 if layer(i) == 0 else 12 for i in range(j % NST, j + 1, NST))

        def rows_count(j):
            return 16 * sum(4 if layer(i) == 0 else 2 for i in range(j + 1))

        def region_of(unit):
            first = unit0(B)
            return unit // 4 if unit < first else 4 * B + (unit - first) // 2

        w1f = W1[:, :].bitcast(F32)

        def ffn_up(l, which, dt, i):
            if l == 0:
                o = which * DT * I0 + dt * I0 + i * P
                return W0[:, o:o + P]
            o = which * DT * I1 + dt * I1 + i * P
            return w1f[:, o:o + rows(l, i)]

        def ffn_down(l, i):
            o = (2 * DT * I0 if l == 0 else 2 * DT * I1) + i * D
            w = W0 if l == 0 else w1f
            return w[0:rows(l, i), o:o + D]

        def rows(l, i):
            return min(P, (I0, I1)[l] - i * P)

        def stacked(j, g):
            if layer(j) == 0:
                return 64 * (g % 2), g // 2, 4 * (g // 2)
            return 0, g, 2 * g

        def keys(j):
            return KS0 if layer(j) == 0 else KS1

        @block.sync
        def _(sp):
            sp.dma_start(XT[:, 0, :, :], xt[0].rearrange("(t p) s -> p t s", p=P)).then_inc(ld_x0, 16)
            sp.dma_start(WQ[0][:, :, :], wq0.rearrange("(t p) n -> p t n", p=P)).then_inc(ld_w0, 16)
            sp.dma_start(WK[0][:, :, :], wk0.rearrange("(t p) n -> p t n", p=P)).then_inc(ld_w0, 16)
            sp.dma_start(WV[0][:, :, :], wv0.rearrange("(t p) n -> p t n", p=P)).then_inc(ld_w0, 16)
            for b in range(1, B):
                sp.dma_start(XT[:, b, :, :], xt[b].rearrange("(t p) s -> p t s", p=P)).then_inc(ld_x, 16)
            raw = [gate0, up0, down0]

            def load_raw(c):
                if c >= 1:
                    sp.wait_ge(q8_used, c)
                w, half = raw[c // 2], c % 2
                if c < 4:
                    src = w[half * P:(half + 1) * P, :]
                    sp.dma_start(RAW[:, :], src).then_inc(ld_raw, 16)
                else:
                    src = w[half * 3 * P:(half + 1) * 3 * P, :].rearrange("(t p) n -> p t n", p=P)
                    sp.dma_start(RAW[:, :].rearrange("p (t n) -> p t n", t=3), src).then_inc(ld_raw, 16)

            for step in steps:
                kind = step[0]
                if kind == "q":
                    j = step[1]
                    sp.wait_ge(q_parts, j + 1)
                    sp.dma_start(dq[j].rearrange("a (m p) s -> p a m s", p=P),
                                 QP[:, :, :].rearrange("p a (m s) -> p a m s", m=2)).then_inc(dq_wr, 16)
                    sp.wait_ge(dq_wr, 16 * (j + 1))
                    if j >= NST:
                        sp.wait_ge(score_mm, 2 * unit0(j - NST + 1))
                    dh, n = DH[layer(j)], 16
                    for half in range(2 if layer(j) == 0 else 1):
                        for i, part in enumerate(Q_PART):
                            lo = 64 * half + dh * i
                            r0 = half * n * dh
                            sp.dma_start(QS[lo:lo + dh, j % NST, :, :],
                                         dq[j, part, r0:r0 + n * dh, :].rearrange("(h d) s -> d h s", d=dh)
                                         ).then_inc(stack_in[j % NST], 16)
                elif kind == "kv":
                    j = step[1]
                    dh = DH[layer(j)]
                    nk = KV[layer(j)] * dh
                    sp.wait_ge(k_parts, j + 1)
                    sp.dma_start(dk[j, :, 0:nk, :].rearrange("a p s -> p a s"),
                                 KP[0:nk, :, :]).then_inc(dk_wr, 16)
                    sp.wait_ge(dk_wr, 16 * (j + 1))
                    ks, n = keys(j), (4 if layer(j) == 0 else 8)
                    if j == 0:
                        sp.wait_ge(ones_dve, 1)
                    for half in range(2 if layer(j) == 0 else 1):
                        for i, part in enumerate(K_PART):
                            lo = 64 * half + dh * i
                            r0 = half * n * dh
                            sp.dma_start(ks[lo:lo + dh, j % NST, :, :],
                                         dk[j, part, r0:r0 + n * dh, :].rearrange("(h d) s -> d h s", d=dh)
                                         ).then_inc(stack_in[j % NST], 16)
                    if j == 0:
                        sp.dma_start(X[:, :, :, :].rearrange("p b t d -> p (b t) d"),
                                     x.rearrange("b (t p) d -> p (b t) d", p=P)).then_inc(ld_s, 16)
                        sp.dma_start(WO[0][:, :, :], wo0.rearrange("(t p) n -> p t n", p=P)).then_inc(ld_s, 16)
                        sp.dma_start(DS[:, :], ds0.broadcast_to((P, D))).then_inc(ld_s, 16)
                        sp.dma_start(GS[:, :], gs0).then_inc(ld_s, 16)
                        sp.dma_start(US[:, :], us0).then_inc(ld_s, 16)
                        sp.dma_start(LT[:, :], lut.broadcast_to((P, LUT))).then_inc(ld_s, 16)
                        load_raw(0)
                    if j == 1:
                        sp.wait_ge(const_pool, 1)
                        sp.dma_start(W1[:, 0:DT * I1].rearrange("p (t n) -> p t n", t=DT),
                                     gidx.rearrange("(t p) n -> p t n", p=P)).then_inc(ld_idx, 16)
                        sp.dma_start(W1[:, DT * I1:2 * DT * I1].rearrange("p (t n) -> p t n", t=DT),
                                     uidx.rearrange("(t p) n -> p t n", p=P)).then_inc(ld_idx, 16)
                        o = 2 * DT * I1
                        sp.dma_start(W1[:, o:o + 5 * D].rearrange("p (t n) -> p t n", t=5),
                                     didx[0:5 * P, :].rearrange("(t p) n -> p t n", p=P)).then_inc(ld_idx, 16)
                        sp.dma_start(W1[0:I1 - 5 * P, o + 5 * D:], didx[5 * P:, :]).then_inc(ld_idx, 16)
                        sp.dma_start(WQ[1][:, :, :], wq1.rearrange("(t p) n -> p t n", p=P)).then_inc(ld_w1, 16)
                        sp.dma_start(WK[1][:, :, :], wk1.rearrange("(t p) n -> p t n", p=P)).then_inc(ld_w1, 16)
                        sp.dma_start(WV[1][:, :, :], wv1.rearrange("(t p) n -> p t n", p=P)).then_inc(ld_w1, 16)
                        sp.dma_start(WO[1][:, :, :], wo1.rearrange("(t p) n -> p t n", p=P)).then_inc(ld_w1, 16)
                elif kind == "mt":
                    j = step[1]
                    sp.wait_ge(m_parts, j + 1)
                    r = STACK[layer(j)]
                    for half in range(2 if layer(j) == 0 else 1):
                        for part in range(2):
                            row = 64 * half + r + part
                            sp.dma_start(QS[row:row + 1, j % NST, :, :],
                                         MP[16 * half:16 * half + 16, part, :]).then_inc(m_rows, 16)
                elif kind == "bounce":
                    _, j, p = step
                    n = 2 * j + p
                    l = layer(j)
                    a, w = (8, 16) if l == 0 else (4, 32)
                    sp.wait_ge(staged, n + 1)
                    sp.dma_start(do[j, p], ST[:, n % 2, :]).then_inc(do_wr, 16)
                    sp.wait_ge(do_wr, 16 * (n + 1))
                    src = do[j, p].rearrange("(a w) (r s) -> r a w s", w=w, r=2)
                    for r in range(2):
                        sp.dma_start(SUMS[64 * r:64 * r + 64, n % 2, 0:32 * a // 8],
                                     src[r, :, DH[l], :].rearrange("a (c s) -> a c s", c=64 // a)
                                     ).then_inc(sums_in, 16)
                    if n >= 2:
                        sp.wait_ge(normed, n - 1)
                    for r in range(2):
                        sp.dma_start(OP[64 * r:64 * r + 64, j % 2, p, :],
                                     src[r, :, 0:DH[l], :]).then_inc(o_in[n % 2], 16)
                elif kind == "recip":
                    _, j, p = step
                    n = 2 * j + p
                    a = 8 if layer(j) == 0 else 4
                    sp.wait_ge(recip_done, n + 1)
                    sp.dma_start(dr[j, p, 0:512 * a].rearrange("(q s) -> q s", q=P),
                                 RCP[:, n % 2, 0:32 * a // 8]).then_inc(dr_wr, 16)
                    sp.wait_ge(dr_wr, 16 * (n + 1))
                    dh = DH[layer(j)]
                    sp.dma_start(OR[:, j % 2, p, :],
                                 dr[j, p, 0:512 * a].rearrange("(h o s) -> h o s", s=S, o=1)
                                 .broadcast_to((2 * a, dh, S))).then_inc(o_in[n % 2], 16)
                elif kind == "q8":
                    if step[1] + 1 < N_Q8:
                        load_raw(step[1] + 1)
                elif kind == "out":
                    j = step[1]
                    sp.wait_ge(x_new, norms[("down", j)] + 1)
                    sp.dma_start(out[j - B].rearrange("(t p) d -> p t d", p=P),
                                 X[:, j - B, :, :]).then_inc(out_wr, 16)
            sp.wait_ge(out_wr, 16 * B)

        @block.gpsimd
        def _(pool):
            own = [0]

            def link(ins):
                own[0] += 1
                ins.then_inc(pool_own, 1)
                pool.wait_ge(pool_own, own[0])

            pool.memset(W1[:, 2 * DT * I1 + 5 * D:], 0).then_inc(const_pool, 1)
            pool.memset(IDN[:, :], 0.0).then_inc(idn_zero, 1)
            pool.wait_ge(idn_zero, 1)
            pool.affine_select(out=IDN[:, :], in_=IDN[:, :], compare_op=ALU.not_equal, fill=1.0,
                               base=0, pattern=[[-1, P]], channel_multiplier=1).then_inc(const_pool, 1)
            link(pool.memset(NHALF[:, :], -0.5))

            for step in steps:
                kind = step[0]
                if kind in ("q", "kv"):
                    j = step[1]
                    wait_free(pool, fill[step])
                    if kind == "q":
                        parts, rem, done, n, wr = QP, QR, q_parts, P, dq_wr
                    else:
                        parts, rem, done, n, wr = KP, KR, k_parts, KV[layer(j)] * DH[layer(j)], dk_wr
                    if j >= 1:
                        pool.wait_ge(wr, 16 * j)
                    link(pool.tensor_copy(parts[0:n, 1, :], rem[0:n, :]))
                    pool.tensor_tensor(parts[0:n, 2, :], rem[0:n, :], parts[0:n, 1, :],
                                       ALU.subtract).then_inc(done, 1)
                elif kind == "norm":
                    _, j, p = step
                    n = 2 * j + p
                    pool.wait_ge(o_in[n % 2], 48 * (n // 2 + 1))
                    if j >= 2:
                        pool.wait_ge(fill_ready, fill[("wo", j - 2)] + 1)
                    pool.tensor_tensor(ON[:, j % 2, p, :], OP[:, j % 2, p, :], OR[:, j % 2, p, :],
                                       ALU.mult).then_inc(normed, 1)
                elif kind in ("wo", "down"):
                    b = step[1] % B
                    pool.wait_ge(mv_done, norms[step] + 1)
                    link(pool.tensor_scalar(VE[:, :], MV[:, :, 1], 1.0, EPS, ALU.mult, ALU.add))
                    link(pool.tensor_tensor(RSTD[:, :], VE[:, :], NHALF[:, :], ALU.pow))
                    for t in range(TT):
                        link(pool.tensor_scalar(NMR[:, t:t + 1], MV[:, t, 0:1], RSTD[:, t:t + 1], -1.0,
                                                ALU.mult, ALU.mult))
                    for t in range(TT):
                        ins = pool.tensor_scalar(X[:, b, t, :], X[:, b, t, :], RSTD[:, t:t + 1],
                                                 NMR[:, t:t + 1], ALU.mult, ALU.add)
                    ins.then_inc(x_new, 1)
                elif kind == "lutmask":
                    c = step[1]
                    pool.wait_ge(bit_done, c + 1)
                    for i in range(LUT // 2):
                        ins = pool.tensor_scalar(LV[:, i, :], LB0[:, :], LD[:, i:i + 1],
                                                 LT[:, 2 * i:2 * i + 1], ALU.mult, ALU.add)
                    ins.then_inc(level1, 1)

        @block.scalar
        def _(act):
            for step in steps:
                kind = step[0]
                if kind in ("q", "kv", "mt", "tr", "gu"):
                    n = fill[step]
                    bank = FB[n % 2]
                    act.wait_ge(fill_ready, n + 1)
                if kind == "q":
                    j = step[1]
                    if j >= 1:
                        act.wait_ge(dq_wr, 16 * j)
                    act.activation(QP[:, 0, :], bank[:, :], ACT.Copy).then_inc(q_hi, 1)
                elif kind == "kv":
                    j = step[1]
                    l = layer(j)
                    nv = KV[l] * DH[l]
                    if j == 0:
                        act.wait_ge(ones_dve, 2)
                    if j >= NST:
                        act.wait_ge(pv_mm, 4 * (j - NST + 1))
                    for kt in range(2):
                        src = bank[:, S + kt * nv:S + (kt + 1) * nv].rearrange("p (g d) -> p g d", g=8)
                        dst = VP0[:, j % NST, kt, :, 16:24] if l == 0 else VP1[:, j % NST, kt, :, 0:16]
                        act.activation(dst, src, ACT.Copy)
                    if j >= 1:
                        act.wait_ge(dk_wr, 16 * j)
                    act.activation(KP[0:nv, 0, :], bank[0:nv, 0:S], ACT.Copy).then_inc(k_hi, 1)
                elif kind == "mt":
                    j = step[1]
                    h = HEADS[layer(j)]
                    if j >= 1:
                        act.wait_ge(m_rows, rows_count(j - 1))
                    act.activation(MP[0:h, 0, :], bank[0:h, 0:S], ACT.Copy, scale=-1.0).then_inc(m_hi, 1)
                elif kind == "tr":
                    b = step[1] % B
                    act.activation(XT[:, b, :, :].rearrange("p t s -> p (t s)"), bank[:, :],
                                   ACT.Copy).then_inc(fill_free[n % 2], 1)
                elif kind == "gu":
                    _, j, i = step
                    r = rows(layer(j), i)
                    if layer(j) == 0:
                        if i == 0:
                            act.wait_ge(scales_dve, 1)
                        scale = GSH[:, i:i + 1]
                    else:
                        scale = 0.5
                    c = 6 * j + i
                    if c >= 2:
                        before = ("gu", (c - 2) // 6, (c - 2) % 6)
                        wait_free(act, fill[before])
                    act.activation(TH[0:r, c % 2, :], bank[0:r, 0:S], ACT.Tanh,
                                   scale=scale[0:r] if layer(j) == 0 else scale).then_inc(th_done, 1)
                elif kind == "score":
                    _, j, u = step
                    unit = unit0(j) + u
                    if unit >= PB_UNITS:
                        act.wait_ge(pv_mm, region_of(unit - PB_UNITS) + 1)
                    for kt in range(2):
                        n = 2 * unit + kt
                        act.wait_ge(score_mm, n + 1)
                        act.activation(PB[:, unit % PB_UNITS, kt, :, :], SC[n % 3][:, :, :], ACT.Exp,
                                       scale=DH[layer(j)] ** -0.5).then_inc(exp_done, 1)
                elif kind == "bounce":
                    _, j, p = step
                    n = 2 * j + p
                    act.wait_ge(pv_mm, 2 * (n + 1))
                    if n >= 2:
                        act.wait_ge(do_wr, 16 * (n - 1))
                    act.activation(ST[:, n % 2, :], PV[:, :, :].rearrange("p r s -> p (r s)"),
                                   ACT.Copy).then_inc(staged, 1)
                elif kind == "q8":
                    c = step[1]
                    act.wait_ge(ld_raw, 16 * (c + 1))
                    if c >= 1:
                        act.wait_ge(q8_used, c)
                    act.activation(Q8A[:, :], RAW[:, :], ACT.Copy, saturate=False)
                    act.activation(Q8B[:, :], RAW[:, :], ACT.Copy, scale=0.25,
                                   saturate=False).then_inc(q8_cast, 1)

        @block.vector
        def _(dve):
            own = [0]

            def link(ins):
                own[0] += 1
                ins.then_inc(dve_own, 1)
                dve.wait_ge(dve_own, own[0])

            dve.memset(KS1[:, :, :, :], 1.0)
            dve.memset(KS0[:, :, :, :], 1.0).then_inc(ones_dve, 1)
            link(dve.memset(VP0[:, :, :, :, :], 0.0))
            dve.memset(VP0[:, :, :, :, 24:25], 1.0)
            link(dve.memset(VP1[:, :, :, :, :], 0.0))
            dve.memset(VP1[:, :, :, :, 16:17], 1.0).then_inc(ones_dve, 1)

            def layer_norm(b, step):
                if norms[step] >= 1:
                    dve.wait_ge(x_new, norms[step])
                for t in range(TT):
                    ins = dve.bn_stats(BST[:, t, :], X[:, b, t, :])
                link(ins)
                for t in range(TT):
                    ins = dve.bn_aggr(MV[:, t, :], BST[:, t, :])
                ins.then_inc(mv_done, 1)

            for step in steps:
                kind = step[0]
                if kind in FILL:
                    n = fill[step]
                    bank = FB[n % 2]
                if kind == "q":
                    j = step[1]
                    dve.wait_ge(q_hi, j + 1)
                    if j >= 1:
                        dve.wait_ge(q_parts, j)
                    dve.tensor_tensor(QR[:, :], bank[:, :], QP[:, 0, :],
                                      ALU.subtract).then_inc(fill_free[n % 2], 1)
                elif kind == "kv":
                    j = step[1]
                    nk = KV[layer(j)] * DH[layer(j)]
                    dve.wait_ge(k_hi, j + 1)
                    if j >= 1:
                        dve.wait_ge(k_parts, j)
                    dve.tensor_tensor(KR[0:nk, :], bank[0:nk, 0:S], KP[0:nk, 0, :],
                                      ALU.subtract).then_inc(fill_free[n % 2], 1)
                elif kind == "max":
                    _, j, u = step
                    if u == 0 and j >= 2:
                        dve.wait_ge(fill_ready, fill[("mt", j - 2)] + 1)
                    for e in range(2):
                        m = 2 * (unit0(j) + u) + e
                        if layer(j) == 0:
                            g, qt = u // 2, u % 2
                            col = 16 * (g % 2) + 4 * (g // 2) + 2 * e
                        else:
                            qt = u % 2
                            col = 4 * (u // 2) + 2 * e
                        dve.wait_ge(max_mm, m + 1)
                        dve.tensor_reduce(MX[:, j % 2, qt, col:col + 2], MM[m % 2][:, :, :],
                                          axis=AX.X, op=ALU.max).then_inc(max_red, 1)
                elif kind == "mt":
                    j = step[1]
                    h = HEADS[layer(j)]
                    dve.wait_ge(m_hi, j + 1)
                    link(dve.scalar_tensor_tensor(out=MP[0:h, 1, :], in0=bank[0:h, 0:S], scalar=-1.0,
                                                  in1=MP[0:h, 0, :], op0=ALU.mult, op1=ALU.subtract))
                    dve.sem_inc(m_parts, 1)
                    dve.sem_inc(fill_free[n % 2], 1)
                elif kind == "recip":
                    _, j, p = step
                    m = 2 * j + p
                    w = 32 if layer(j) == 0 else 16
                    dve.wait_ge(sums_in, 32 * (m + 1))
                    if m >= 2:
                        dve.wait_ge(dr_wr, 16 * (m - 1))
                    dve.reciprocal(RCP[:, m % 2, 0:w], SUMS[:, m % 2, 0:w]).then_inc(recip_done, 1)
                elif kind == "wo":
                    j = step[1]
                    b = j % B
                    dve.wait_ge(fill_ready, n + 1)
                    if j == 0:
                        dve.wait_ge(ld_s, 16 * 6)
                    x2 = X[:, b, :, :].rearrange("p t d -> p (t d)")
                    dve.tensor_tensor(x2, bank[:, :], x2, ALU.add).then_inc(fill_free[n % 2], 1)
                    wait_free(dve, n)
                    layer_norm(b, step)
                elif kind == "down":
                    j = step[1]
                    b = j % B
                    x2 = X[:, b, :, :].rearrange("p t d -> p (t d)")
                    dve.wait_ge(fill_ready, n + 1)
                    if layer(j) == 0:
                        for t in range(TT):
                            ins = dve.tensor_tensor(YD[:, t, :], bank[:, t * D:(t + 1) * D], DS[:, :], ALU.mult)
                        ins.then_inc(fill_free[n % 2], 1)
                        wait_free(dve, n)
                        link(dve.tensor_tensor(x2, YD[:, :, :].rearrange("p t d -> p (t d)"), x2, ALU.add))
                    else:
                        dve.tensor_tensor(x2, bank[:, :], x2, ALU.add).then_inc(fill_free[n % 2], 1)
                        wait_free(dve, n)
                    layer_norm(b, step)
                elif kind == "gu":
                    _, j, i = step
                    r = rows(layer(j), i)
                    dve.wait_ge(th_done, 6 * j + i + 1)
                    if i == 0 and j >= 1:
                        dve.wait_ge(fill_ready, fill[("down", j - 1)] + 1)
                    if 6 * j + i >= 1:
                        wait_free(dve, fill["gu", (6 * j + i - 1) // 6, (i + 5) % 6])
                    link(dve.scalar_tensor_tensor(out=AA[0:r, :], in0=TH[0:r, (6 * j + i) % 2, :], scalar=1.0,
                                                  in1=bank[0:r, 0:S], op0=ALU.add, op1=ALU.mult))
                    c = GUS[0:r, i:i + 1] if layer(j) == 0 else 0.5
                    dve.scalar_tensor_tensor(out=HT[0:r, i, :], in0=bank[0:r, S:2 * S], scalar=c,
                                             in1=AA[0:r, :], op0=ALU.mult,
                                             op1=ALU.mult).then_inc(fill_free[n % 2], 1)
                elif kind == "q8":
                    c = step[1]
                    if c == 0:
                        dve.wait_ge(ld_s, 16 * 6)
                        link(dve.tensor_scalar(GSH[:, :], GS[:, :], 0.5, None, ALU.mult))
                        dve.tensor_tensor(GUS[:, :], GSH[:, :], US[:, :], ALU.mult).then_inc(scales_dve, 1)
                        dve.tensor_tensor(LD[:, :], LT[:, 1:LUT:2], LT[:, 0:LUT:2], ALU.subtract)
                    w = W0[:, c * Q8_W:(c + 1) * Q8_W]
                    dve.wait_ge(q8_cast, c + 1)
                    link(dve.tensor_scalar(BIG[:, :], RAW[:, :], 1.0, None, ALU.is_ge))
                    dve.scalar_tensor_tensor(out=BIG[:, :], in0=RAW[:, :], scalar=-1.0, in1=BIG[:, :],
                                             op0=ALU.is_le, op1=ALU.add)
                    dve.tensor_copy(w, Q8A[:, :])
                    link(dve.tensor_scalar(QB[:, :], Q8B[:, :], 4.0, None, ALU.mult))
                    dve.copy_predicated(w, BIG[:, :], QB[:, :]).then_inc(q8_used, 1)
                    dve.wait_ge(q8_used, c + 1)
                elif kind == "lutmask":
                    c = step[1]
                    if c == 0:
                        dve.wait_ge(ld_idx, 16 * 4)
                    src = W1[:, c * LUT_W:(c + 1) * LUT_W]
                    for k in range(4):
                        ins = dve.tensor_scalar(LB[:, k, :], src, 1 << k, None, ALU.bitwise_and)
                        if k == 0:
                            link(ins)
                    dve.tensor_copy(LB0[:, :], LB[:, 0, :]).then_inc(bit_done, 1)
                elif kind == "lutpick":
                    c = step[1]
                    dve.wait_ge(level1, c + 1)
                    for k in (1, 2, 3):
                        gap = 1 << (k - 1)
                        for i in range(0, LUT // 2, 2 * gap):
                            ins = dve.copy_predicated(LV[:, i, :], LB[:, k, :], LV[:, i + gap, :])
                        link(ins)
                    link(dve.tensor_copy(w1f[:, c * LUT_W:(c + 1) * LUT_W], LV[:, 0, :]))
                    dve.sem_inc(lut_done, 1)

        @block.tensor
        def _(pe):
            for step in steps:
                kind = step[0]
                if kind in FILL:
                    n = fill[step]
                    bank = FB[n % 2]
                    if n >= 2:
                        wait_free(pe, n - 2)
                if kind == "q":
                    j = step[1]
                    l, b = layer(j), j % B
                    if l == 0:
                        pe.wait_ge(ld_x0, 16)
                        if b >= 1:
                            pe.wait_ge(ld_x, 16 * (B - 1))
                        pe.wait_ge(ld_w0, 16 * 3)
                    else:
                        wait_free(pe, fill[("tr", j - B, 1)])
                        pe.wait_ge(ld_w1, 16 * 4)
                    for m in range(2):
                        for t in range(DT):
                            ins = pe.matmul(bank[:, m * S:(m + 1) * S], WQ[l][:, t, m * P:(m + 1) * P],
                                            XT[:, b, t, :], start=t == 0, stop=t == DT - 1)
                    ins.then_inc(fill_ready, 1)
                elif kind == "kv":
                    j = step[1]
                    l, b = layer(j), j % B
                    nv = KV[l] * DH[l]
                    for t in range(DT):
                        pe.matmul(bank[0:nv, 0:S], WK[l][:, t, :], XT[:, b, t, :],
                                  start=t == 0, stop=t == DT - 1)
                    for kt in range(2):
                        for t in range(DT):
                            ins = pe.matmul(bank[:, S + kt * nv:S + (kt + 1) * nv],
                                            XT[:, b, t, kt * P:(kt + 1) * P], WV[l][:, t, :],
                                            start=t == 0, stop=t == DT - 1)
                    ins.then_inc(fill_ready, 1)
                elif kind == "max":
                    _, j, u = step
                    if u == 0:
                        pe.wait_ge(stack_in[j % NST], stack_count(j))
                    r = STACK[layer(j)]
                    for e in range(2):
                        m = 2 * (unit0(j) + u) + e
                        if m >= 2:
                            pe.wait_ge(max_red, m - 1)
                        for i in range(2):
                            if layer(j) == 0:
                                g, qt, h = u // 2, u % 2, 2 * e + i
                            else:
                                g, qt, h = 2 * (u // 2) + e, u % 2, i
                            lo, ks, qs = stacked(j, g)
                            ins = pe.matmul(MM[m % 2][:, i, :],
                                            QS[lo:lo + r, j % NST, qs + h, qt * P:(qt + 1) * P],
                                            keys(j)[lo:lo + r, j % NST, ks, :], start=True, stop=True)
                        ins.then_inc(max_mm, 1)
                elif kind == "mt":
                    j = step[1]
                    h = HEADS[layer(j)]
                    pe.wait_ge(max_red, 2 * unit0(j + 1))
                    pe.wait_ge(const_pool, 2)
                    for qt in range(2):
                        ins = pe.transpose(bank[0:h, qt * P:(qt + 1) * P], MX[:, j % 2, qt, 0:h], IDN[:, :])
                    ins.then_inc(fill_ready, 1)
                elif kind == "score":
                    _, j, u = step
                    if u == 0:
                        pe.wait_ge(m_rows, rows_count(j))
                    r = STACK[layer(j)] + 2
                    if layer(j) == 0:
                        g, h = 4 * (u // 8) + u % 4, 2 * ((u // 4) % 2)
                    else:
                        g, h = u, 0
                    lo, ks, qs = stacked(j, g)
                    for kt in range(2):
                        n = 2 * (unit0(j) + u) + kt
                        if n >= 3:
                            pe.wait_ge(exp_done, n - 2)
                        pe.matmul(SC[n % 3][:, :, :],
                                  keys(j)[lo:lo + r, j % NST, ks, kt * P:(kt + 1) * P],
                                  QS[lo:lo + r, j % NST, qs + h:qs + h + 2, :],
                                  start=True, stop=True).then_inc(score_mm, 1)
                elif kind == "pv":
                    _, j, r = step
                    per = UNITS[layer(j)] // 4
                    first = unit0(j) + per * r
                    pe.wait_ge(exp_done, 2 * (first + per))
                    if r % 2 == 0 and j + r > 0:
                        pe.wait_ge(staged, 2 * j + r // 2)
                    if layer(j) == 0:
                        for kt in range(2):
                            for e in range(2):
                                for c in range(4):
                                    w = 16 - 16 * e
                                    ins = pe.matmul(PV[32 * c:32 * c + 32, r % 2, :],
                                                    VP0[:, j % NST, kt, 4 * (r // 2) + c, w:w + 32],
                                                    PB[:, (first + c) % PB_UNITS, kt, e, :],
                                                    start=kt + e == 0, stop=kt + e == 2)
                    else:
                        for kt in range(2):
                            for c in range(4):
                                ins = pe.matmul(PV[32 * c:32 * c + 32, r % 2, :],
                                                VP1[:, j % NST, kt, 2 * r + c // 2, :],
                                                PB[:, (first + c // 2) % PB_UNITS, kt, c % 2, :],
                                                start=kt == 0, stop=kt == 1)
                    ins.then_inc(pv_mm, 1)
                elif kind == "wo":
                    j = step[1]
                    if j == 0:
                        pe.wait_ge(ld_s, 16 * 6)
                    pe.wait_ge(normed, 2 * (j + 1))
                    for t in range(TT):
                        for p in range(2):
                            ins = pe.matmul(bank[:, t * D:(t + 1) * D], ON[:, j % 2, p, t * P:(t + 1) * P],
                                            WO[layer(j)][:, p, :], start=p == 0, stop=p == 1)
                    ins.then_inc(fill_ready, 1)
                elif kind == "tr":
                    _, j, w = step
                    pe.wait_ge(x_new, norms[("wo", "down")[w], j] + 1)
                    for d in range(DT):
                        for t in range(TT):
                            ins = pe.transpose(bank[:, d * S + t * P:d * S + (t + 1) * P],
                                               X[:, j % B, t, d * P:(d + 1) * P], IDN[:, :])
                    ins.then_inc(fill_ready, 1)
                elif kind == "gu":
                    _, j, i = step
                    l, b = layer(j), j % B
                    r = rows(l, i)
                    if i == 0:
                        wait_free(pe, fill[("tr", j, 0)])
                        if l == 0:
                            pe.wait_ge(q8_used, N_Q8)
                        else:
                            pe.wait_ge(lut_done, N_LUT)
                    for w in range(2):
                        for t in range(DT):
                            ins = pe.matmul(bank[0:r, w * S:(w + 1) * S], ffn_up(l, w, t, i),
                                            XT[:, b, t, :], start=t == 0, stop=t == DT - 1)
                    ins.then_inc(fill_ready, 1)
                elif kind == "down":
                    j = step[1]
                    l = layer(j)
                    for i in range(4, 6):
                        wait_free(pe, fill[("gu", j, i)])
                    for t in range(TT):
                        for i in range(6):
                            r = rows(l, i)
                            ins = pe.matmul(bank[:, t * D:(t + 1) * D], HT[0:r, i, t * P:(t + 1) * P],
                                            ffn_down(l, i), start=i == 0, stop=i == 5)
                    ins.then_inc(fill_ready, 1)


def build(nc, args):
    two_layer_kernel(nc, *args)


def kernel(**inputs):
    import numpy as np
    import concourse.bacc as bacc
    from concourse.bass_utils import run_bass_kernel_spmd

    a = {k: np.asarray(v) for k, v in inputs.items()}
    dh0 = D // 32
    wq0 = a["L0_attn_Wq"].reshape(D, 4, 2, 4, dh0).transpose(0, 2, 1, 3, 4).reshape(D, D)
    wk0 = a["L0_attn_Wk"].reshape(D, 4, 2, dh0).transpose(0, 2, 1, 3).reshape(D, 64)
    wo0 = a["L0_attn_Wo"].reshape(2, 4, 2, 2, dh0, D).transpose(0, 2, 1, 3, 4, 5).reshape(D, D)
    arrays = {
        "x": a["L0_attn_x"],
        "xt": a["L0_attn_x"].transpose(0, 2, 1),
        "wq0": wq0, "wk0": wk0, "wv0": a["L0_attn_Wv"], "wo0": wo0,
        "gate0": a["L0_ffn_gate_w"], "up0": a["L0_ffn_up_w"], "down0": a["L0_ffn_down_w"],
        "gs0": a["L0_ffn_gate_scale"].reshape(6, P).T, "us0": a["L0_ffn_up_scale"].reshape(6, P).T,
        "ds0": a["L0_ffn_down_scale"].reshape(1, D),
        "wq1": a["L1_attn_wq"].T, "wk1": a["L1_attn_wk"].T, "wv1": a["L1_attn_wv"].T,
        "wo1": a["L1_attn_wo"].T,
        "lut": a["L1_ffn_lut"].reshape(1, LUT),
        "gidx": a["L1_ffn_gate_idx"].T, "uidx": a["L1_ffn_up_idx"].T, "didx": a["L1_ffn_down_idx"].T,
    }
    nc = bacc.Bacc("TRN2", target_bir_lowering=False, num_devices=1)
    feeds, args = {}, []
    for name, v in arrays.items():
        v = np.ascontiguousarray(v)
        feeds["in_" + name] = v
        args.append(nc.dram_tensor("in_" + name, v.shape, mybir.dt.from_np(v.dtype), kind="ExternalInput").ap())
    args.append(nc.dram_tensor("out_0", (B, S, D), F32, kind="ExternalOutput").ap())
    build(nc, args)
    r = run_bass_kernel_spmd(nc, [feeds], core_ids=[0])
    return r.results[0]["out_0"]
```

```python
from contextlib import ExitStack

import concourse.bass as bass
from concourse import mybir

P = 128
F32 = mybir.dt.float32
BF16 = mybir.dt.bfloat16
FP8 = mybir.dt.float8e4
I32 = mybir.dt.int32
ALU = mybir.AluOpType
ACT = mybir.ActivationFunctionType
AX = mybir.AxisListType

B, S, D = 4, 256, 256
HEADS = (32, 16)
KV = (8, 8)
I0, I1 = 768, 688
LUT = 16
EPS = 1e-5
DH = tuple(D // h for h in HEADS)
UNITS = tuple(h * 2 * S // 1024 for h in HEADS)
JOBS = 2 * B
DT = D // P
TT = S // P

Q_PART = (0, 0, 0, 1, 1, 2)
K_PART = (0, 1, 2, 0, 1, 0)
NPROD = len(Q_PART)
STACK = tuple(NPROD * d for d in DH)

PB_UNITS = 6
NST = 3
Q8_W = 768
LUT_W = 268
W1_COLS = 2 * DT * I1 + 6 * D
N_Q8 = (2 * DT * I0 + 6 * D) // Q8_W
N_LUT = W1_COLS // LUT_W


def layer(j):
    return j // B


def halves(j):
    return 2 if layer(j) == 0 else 1


def unit0(j):
    return sum(UNITS[layer(i)] for i in range(j))


SLOT = (48.0, 36.0)
LAG = {
    "q": {"ACT": 1.5, "DVE": 2.5, "POOL": 3.5, "SP": 6.0},
    "kv": {"ACT": 1.5, "DVE": 3.0, "POOL": 4.0, "SP": 6.5},
    "max": {"DVE": 0.7},
    "mt": {"ACT": 1.0, "DVE": 1.5, "SP": 2.0},
    "score": {"ACT": 0.7},
    "pv": {},
    "bounce": {"ACT": 0.0, "SP": 1.0},
    "recip": {},
    "spread": {},
    "norm": {},
    "wo": {"DVE": 2.0, "POOL": 4.0},
    "tr": {"ACT": 1.0},
    "gu": {"ACT": 2.0, "DVE": 2.6},
    "down": {"DVE": 5.0, "POOL": 7.5},
    "out": {},
    "q8": {"SP": 0.0, "ACT": 0.5, "DVE": 3.0},
    "lutbits": {"SP": 0.0, "DVE": 0.1},
    "lut1": {},
    "lut2": {}, "lut3": {}, "lut4": {},
}


def plan():
    start = [0.0]
    for j in range(JOBS):
        start.append(start[j] + SLOT[layer(j)])
    at = []
    for j in range(JOBS):
        n, t0, t1, length = UNITS[layer(j)], start[j], start[j + 1], SLOT[layer(j)]
        before = start[j - 1] if j else -40.0
        span = t0 - before
        for u in range(n):
            at.append((t0 + length * (u + 0.5) / n, ("score", j, u)))
            at.append((before + 0.74 * span * (u + 0.3) / n, ("max", j, u)))
        at.append((before + 0.78 * span, ("mt", j)))
        for r in range(4):
            at.append((t0 + length * (r + 1) / 4 + 2.0, ("pv", j, r)))
        for p in range(2):
            t = t0 + length * (p + 1) / 2 + 3.0
            at.append((t, ("bounce", j, p)))
            at.append((t + 7.0, ("recip", j, p)))
            at.append((t + 7.5, ("spread", j, p)))
            at.append((t + 12.0, ("norm", j, p)))
        at.append((t1 + 17.0, ("wo", j)))
        at.append((t1 + 26.0, ("tr", j, 0)))
        for i in range(6):
            at.append((t1 + 28.0 + 2.5 * i, ("gu", j, i)))
        at.append((t1 + 46.0, ("down", j)))
        if layer(j) == 0:
            at.append((t1 + 58.0, ("tr", j, 1)))
            at.append((t1 + 60.0, ("q", j + B)))
            at.append((t1 + 62.0, ("kv", j + B)))
            t = -60.0 if j == 0 else (-40.0, 3.0, start[1] + 3.0)[j - 1]
            at.append((t, ("q", j)))
            at.append((t + 2.0, ("kv", j)))
        else:
            at.append((t1 + 57.0, ("out", j)))
    for c in range(N_Q8):
        at.append((-25.0 + 12.0 * c, ("q8", c)))
    for c in range(N_LUT):
        t = start[1] + 12.0 * c
        at.append((t, ("lutbits", c)))
        for i in range(4):
            at.append((t + 1.0 + 1.5 * i, ("lut1", c, i)))
        for k in (2, 3, 4):
            at.append((t + 6.0 + 1.5 * k, (f"lut{k}", c)))
    return at


def order(engine):
    at = plan()
    return [step for _, step in sorted(at, key=lambda x: x[0] + LAG[x[1][0]].get(engine, 0.0))]


def two_layer_kernel(nc, x, xt, wq0, wk0, wv0, wo0, gate0, up0, down0, gs0, us0, ds0,
                     wq1, wk1, wv1, wo1, lut, gidx, uidx, didx, out):
    steps = order("PE")
    FILL = ("q", "kv", "mt", "wo", "tr", "gu", "down")
    fill = {}
    norms = {}
    trs = {}
    for step in steps:
        if step[0] in FILL:
            fill[step] = len(fill)
        if step[0] in ("wo", "down"):
            norms[step] = len(norms)
        if step[0] == "tr":
            trs[step] = len(trs)

    with ExitStack() as ctx:
        def sb(name, shape, dt=F32):
            return ctx.enter_context(nc.sbuf_tensor(name, shape, dt))

        def pb(name, shape, dt=F32):
            return ctx.enter_context(nc.psum_tensor(name, shape, dt))

        def sem(name):
            return ctx.enter_context(nc.semaphore(name))

        X = sb("X", [P, B, TT, D])
        XT = sb("XT", [P, B, DT, S])
        PB = sb("PB", [P, PB_UNITS, 2, 2, S])
        QS = sb("QS", [P, NST, 16, S], BF16)
        KS0 = sb("KS0", [P, NST, 4, S], BF16)
        KS1 = sb("KS1", [P, NST, 8, S], BF16)
        VP0 = sb("VP0", [P, NST, 2, 8, 48])
        VP1 = sb("VP1", [P, NST, 2, 8, 32])
        QP = sb("QP", [P, 3, 2 * S], BF16)
        QR = sb("QR", [P, 2 * S])
        KP = sb("KP", [P, 3, S], BF16)
        KR = sb("KR", [P, S])
        MX = sb("MX", [P, 2, TT, 32])
        MP = sb("MP", [32, 2, S], BF16)
        ST = sb("ST", [P, 2, 2 * S])
        SUMS = sb("SUMS", [P, 2, 32])
        RCP = sb("RCP", [P, 2, 32])
        OP = sb("OP", [P, 2, 2, S])
        OR = sb("OR", [P, 2, 2, S])
        ON = sb("ON", [P, 2, 2, S])
        WQ = [sb("WQ0", [P, DT, D]), sb("WQ1", [P, DT, D])]
        WK = [sb("WK0", [P, DT, 64]), sb("WK1", [P, DT, 128])]
        WV = [sb("WV0", [P, DT, 64]), sb("WV1", [P, DT, 128])]
        WO = [sb("WO0", [P, 2, D]), sb("WO1", [P, 2, D])]
        HT = sb("HT", [P, 6, S])
        TH = sb("TH", [P, 2, S])
        AA = sb("AA", [P, S])
        W0 = sb("W0", [P, N_Q8 * Q8_W])
        W1 = sb("W1", [P, W1_COLS], I32)
        DS = sb("DS", [P, D])
        YD = sb("YD", [P, TT, D])
        RAW = sb("RAW", [P, Q8_W])
        Q8A = sb("Q8A", [P, Q8_W], FP8)
        Q8B = sb("Q8B", [P, Q8_W], FP8)
        BIG = sb("BIG", [P, Q8_W], I32)
        QB = sb("QB", [P, Q8_W])
        LB = sb("LB", [P, 4, LUT_W], I32)
        LB0 = sb("LB0", [P, LUT_W])
        LV = sb("LV", [P, 8, LUT_W])
        LT = sb("LT", [P, LUT])
        LD = sb("LD", [P, LUT // 2])
        GS = sb("GS", [P, 6])
        US = sb("US", [P, 6])
        GSH = sb("GSH", [P, 6])
        GUS = sb("GUS", [P, 6])
        IDN = sb("IDN", [P, P])
        BST = sb("BST", [P, TT, 6])
        MV = sb("MV", [P, TT, 2])
        RSTD = sb("RSTD", [P, TT])
        VE = sb("VE", [P, TT])
        NMR = sb("NMR", [P, TT])
        NHALF = sb("NHALF", [P, TT])

        SC = [pb(f"SC{i}", [P, 2, S]) for i in range(3)]
        MM = [pb(f"MM{i}", [P, 2, S]) for i in range(2)]
        PV = pb("PV", [P, 2, S])
        FB = [pb(f"FB{i}", [P, 2 * S]) for i in range(2)]

        dq = nc.dram_tensor("dq", (JOBS, 3, D, S), BF16, kind="Internal").ap()
        dk = nc.dram_tensor("dk", (JOBS, 3, P, S), BF16, kind="Internal").ap()
        do = nc.dram_tensor("do", (JOBS, 2, 2, P, S), F32, kind="Internal").ap()
        dr = nc.dram_tensor("dr", (JOBS, 2, 4096), F32, kind="Internal").ap()

        ld_x = sem("ld_x")
        ld_x0 = sem("ld_x0")
        ld_w0 = sem("ld_w0")
        ld_w1 = sem("ld_w1")
        ld_s = sem("ld_s")
        ld_raw = sem("ld_raw")
        ld_idx = sem("ld_idx")
        idn_zero = sem("idn_zero")
        const_pool = sem("const_pool")
        ones_pool = sem("ones_pool")
        scales_dve = sem("scales_dve")
        fill_ready = sem("fill_ready")
        fill_free = [sem(f"fill_free{i}") for i in range(2)]
        q_hi = sem("q_hi")
        k_hi = sem("k_hi")
        q_parts = sem("q_parts")
        k_parts = sem("k_parts")
        dq_wr = sem("dq_wr")
        dk_wr = sem("dk_wr")
        stack_in = [sem(f"stack_in{i}") for i in range(NST)]
        max_mm = sem("max_mm")
        max_red = sem("max_red")
        m_hi = sem("m_hi")
        m_parts = sem("m_parts")
        m_rows = sem("m_rows")
        score_mm = sem("score_mm")
        exp_done = sem("exp_done")
        pv_mm = sem("pv_mm")
        staged = sem("staged")
        do_wr = sem("do_wr")
        sums_in = sem("sums_in")
        recip_done = sem("recip_done")
        dr_wr = sem("dr_wr")
        o_in = [sem(f"o_in{i}") for i in range(2)]
        normed = sem("normed")
        mv_done = sem("mv_done")
        x_new = sem("x_new")
        xt_new = sem("xt_new")
        th_done = sem("th_done")
        q8_cast = sem("q8_cast")
        q8_used = sem("q8_used")
        bit_done = sem("bit_done")
        level1 = sem("level1")
        lut_done = sem("lut_done")
        out_wr = sem("out_wr")
        dve_own = sem("dve_own")
        pool_own = sem("pool_own")
        act_own = sem("act_own")

        block = ctx.enter_context(nc.Block())

        def wait_free(eng, n):
            eng.wait_ge(fill_free[n % 2], n // 2 + 1)

        def stack_count(j):
            return 16 * sum(6 * halves(i) for i in range(j % NST, j + 1, NST))

        def rows_count(j):
            return 16 * sum(2 * halves(i) for i in range(j + 1))

        def region_of(unit):
            first = unit0(B)
            return unit // 4 if unit < first else 4 * B + (unit - first) // 2

        w1f = W1[:, :].bitcast(F32)

        def ffn_up(l, which, dt, i):
            if l == 0:
                o = which * DT * I0 + dt * I0 + i * P
                return W0[:, o:o + P]
            o = which * DT * I1 + dt * I1 + i * P
            return w1f[:, o:o + rows(l, i)]

        def ffn_down(l, i):
            o = (2 * DT * I0 if l == 0 else 2 * DT * I1) + i * D
            w = W0 if l == 0 else w1f
            return w[0:rows(l, i), o:o + D]

        def rows(l, i):
            return min(P, (I0, I1)[l] - i * P)

        def stacked(j, g):
            if layer(j) == 0:
                return 64 * (g % 2), g // 2, 4 * (g // 2)
            return 0, g, 2 * g

        def keys(j):
            return KS0 if layer(j) == 0 else KS1

        @block.sync
        def _(sp):
            sp.dma_start(XT[:, 0, :, :], xt[0].rearrange("(t p) s -> p t s", p=P)).then_inc(ld_x0, 16)
            sp.dma_start(WQ[0][:, :, :], wq0.rearrange("(t p) n -> p t n", p=P)).then_inc(ld_w0, 16)
            sp.dma_start(WK[0][:, :, :], wk0.rearrange("(t p) n -> p t n", p=P)).then_inc(ld_w0, 16)
            sp.dma_start(WV[0][:, :, :], wv0.rearrange("(t p) n -> p t n", p=P)).then_inc(ld_w0, 16)
            for b in range(1, B):
                sp.dma_start(XT[:, b, :, :], xt[b].rearrange("(t p) s -> p t s", p=P)).then_inc(ld_x, 16)
            raw = [gate0, up0, down0]

            def load_raw(c):
                if c >= 1:
                    sp.wait_ge(q8_used, c)
                w, half = raw[c // 2], c % 2
                if c < 4:
                    src = w[half * P:(half + 1) * P, :]
                    sp.dma_start(RAW[:, :], src).then_inc(ld_raw, 16)
                else:
                    src = w[half * 3 * P:(half + 1) * 3 * P, :].rearrange("(t p) n -> p t n", p=P)
                    sp.dma_start(RAW[:, :].rearrange("p (t n) -> p t n", t=3), src).then_inc(ld_raw, 16)

            for step in order("SP"):
                kind = step[0]
                if kind == "q":
                    j = step[1]
                    sp.wait_ge(q_parts, j + 1)
                    sp.dma_start(dq[j].rearrange("a (m p) s -> p a m s", p=P),
                                 QP[:, :, :].rearrange("p a (m s) -> p a m s", m=2)).then_inc(dq_wr, 16)
                    sp.wait_ge(dq_wr, 16 * (j + 1))
                    if j >= NST:
                        sp.wait_ge(score_mm, 2 * unit0(j - NST + 1))
                    for half in range(halves(j)):
                        for i, n in ((0, 3), (3, 2), (5, 1)):
                            dh = DH[layer(j)]
                            lo = 64 * half + dh * i
                            src = dq[j, Q_PART[i]].rearrange("(f o d h) s -> f o d (h s)", f=halves(j), o=1, d=dh)
                            sp.dma_start(QS[lo:lo + dh * n, j % NST, :, :].rearrange("p h s -> p (h s)"),
                                         src[half].broadcast_to((n, dh, 16 * S))
                                         ).then_inc(stack_in[j % NST], 16)
                elif kind == "kv":
                    j = step[1]
                    dh = DH[layer(j)]
                    nk = KV[layer(j)] * dh
                    sp.wait_ge(k_parts, j + 1)
                    sp.dma_start(dk[j, :, 0:nk, :].rearrange("a p s -> p a s"),
                                 KP[0:nk, :, :]).then_inc(dk_wr, 16)
                    sp.wait_ge(dk_wr, 16 * (j + 1))
                    ks = keys(j)
                    if j in (0, B):
                        sp.wait_ge(ones_pool, 1 if j == 0 else 3)
                    for half in range(halves(j)):
                        for i, m in ((0, 3), (3, 2), (5, 1)):
                            lo = 64 * half + dh * i
                            src = dk[j, 0:m, 0:nk, :].rearrange("a (f d h) s -> f a d (h s)", f=halves(j), d=dh)
                            sp.dma_start(ks[lo:lo + dh * m, j % NST, :, :].rearrange("p h s -> p (h s)"),
                                         src[half]).then_inc(stack_in[j % NST], 16)
                    if j == 0:
                        sp.dma_start(X[:, :, :, :].rearrange("p b t d -> p (b t) d"),
                                     x.rearrange("b (t p) d -> p (b t) d", p=P)).then_inc(ld_s, 16)
                        sp.dma_start(WO[0][:, :, :], wo0.rearrange("(t p) n -> p t n", p=P)).then_inc(ld_s, 16)
                        sp.dma_start(DS[:, :], ds0.broadcast_to((P, D))).then_inc(ld_s, 16)
                        sp.dma_start(GS[:, :], gs0).then_inc(ld_s, 16)
                        sp.dma_start(US[:, :], us0).then_inc(ld_s, 16)
                        sp.dma_start(LT[:, :], lut.broadcast_to((P, LUT))).then_inc(ld_s, 16)
                        load_raw(0)
                    if j == 1:
                        sp.wait_ge(const_pool, 1)
                        sp.dma_start(W1[:, 0:DT * I1].rearrange("p (t n) -> p t n", t=DT),
                                     gidx.rearrange("(t p) n -> p t n", p=P)).then_inc(ld_idx, 16)
                        sp.dma_start(W1[:, DT * I1:2 * DT * I1].rearrange("p (t n) -> p t n", t=DT),
                                     uidx.rearrange("(t p) n -> p t n", p=P)).then_inc(ld_idx, 16)
                        o = 2 * DT * I1
                        sp.dma_start(W1[:, o:o + 5 * D].rearrange("p (t n) -> p t n", t=5),
                                     didx[0:5 * P, :].rearrange("(t p) n -> p t n", p=P)).then_inc(ld_idx, 16)
                        sp.dma_start(W1[0:I1 - 5 * P, o + 5 * D:], didx[5 * P:, :]).then_inc(ld_idx, 16)
                        sp.dma_start(WQ[1][:, :, :], wq1.rearrange("(t p) n -> p t n", p=P)).then_inc(ld_w1, 16)
                        sp.dma_start(WK[1][:, :, :], wk1.rearrange("(t p) n -> p t n", p=P)).then_inc(ld_w1, 16)
                        sp.dma_start(WV[1][:, :, :], wv1.rearrange("(t p) n -> p t n", p=P)).then_inc(ld_w1, 16)
                        sp.dma_start(WO[1][:, :, :], wo1.rearrange("(t p) n -> p t n", p=P)).then_inc(ld_w1, 16)
                elif kind == "mt":
                    j = step[1]
                    sp.wait_ge(m_parts, j + 1)
                    r = STACK[layer(j)]
                    for half in range(halves(j)):
                        for part in range(2):
                            row = 64 * half + r + part
                            sp.dma_start(QS[row:row + 1, j % NST, :, :],
                                         MP[16 * half:16 * half + 16, part, :]).then_inc(m_rows, 16)
                elif kind == "bounce":
                    _, j, p = step
                    n = 2 * j + p
                    l = layer(j)
                    a, w = (8, 16) if l == 0 else (4, 32)
                    sp.wait_ge(staged, n + 1)
                    sp.dma_start(do[j, p].rearrange("r p s -> p r s"),
                                 ST[:, n % 2, :].rearrange("p (r s) -> p r s", r=2)).then_inc(do_wr, 16)
                    sp.wait_ge(do_wr, 16 * (n + 1))
                    src = do[j, p].rearrange("r (a w) s -> (r a) w s", w=w)
                    c = 64 // a
                    sp.dma_start(SUMS[:, n % 2, 0:S // c],
                                 src[:, DH[l], :].rearrange("a (c s) -> a c s", c=c)).then_inc(sums_in, 16)
                    if n >= 2:
                        sp.wait_ge(normed, n - 1)
                    sp.dma_start(OP[:, j % 2, p, :], src[:, 0:DH[l], :]).then_inc(o_in[n % 2], 16)
                elif kind == "spread":
                    _, j, p = step
                    n = 2 * j + p
                    a, dh = (8, 8) if layer(j) == 0 else (4, 16)
                    sp.wait_ge(recip_done, n + 1)
                    sp.dma_start(dr[j, p, 0:512 * a].rearrange("(q s) -> q s", q=P),
                                 RCP[:, n % 2, 0:S * a // 64]).then_inc(dr_wr, 16)
                    sp.wait_ge(dr_wr, 16 * (n + 1))
                    sp.dma_start(OR[:, j % 2, p, :],
                                 dr[j, p, 0:512 * a].rearrange("(h o s) -> h o s", s=S, o=1)
                                 .broadcast_to((2 * a, dh, S))).then_inc(o_in[n % 2], 16)
                elif kind == "q8":
                    if step[1] + 1 < N_Q8:
                        load_raw(step[1] + 1)
                elif kind == "out":
                    j = step[1]
                    sp.wait_ge(x_new, norms[("down", j)] + 1)
                    sp.dma_start(out[j - B].rearrange("(t p) d -> p t d", p=P),
                                 X[:, j - B, :, :]).then_inc(out_wr, 16)
            sp.wait_ge(out_wr, 16 * B)

        @block.gpsimd
        def _(pool):
            own = [0]

            def link(ins):
                own[0] += 1
                ins.then_inc(pool_own, 1)
                pool.wait_ge(pool_own, own[0])

            pool.memset(W1[:, 2 * DT * I1 + 5 * D:], 0).then_inc(const_pool, 1)
            pool.memset(IDN[:, :], 0.0).then_inc(idn_zero, 1)
            pool.wait_ge(idn_zero, 1)
            pool.affine_select(out=IDN[:, :], in_=IDN[:, :], compare_op=ALU.not_equal, fill=1.0,
                               base=0, pattern=[[-1, P]], channel_multiplier=1).then_inc(const_pool, 1)
            pool.memset(KS0[:, :, :, :], 1.0).then_inc(ones_pool, 1)
            link(pool.memset(VP0[:, :, :, :, :], 0.0))
            pool.memset(VP0[:, :, :, :, 24:25], 1.0).then_inc(ones_pool, 1)
            link(pool.memset(NHALF[:, :], -0.5))

            def late_constants():
                pool.memset(KS1[:, :, :, :], 1.0)
                link(pool.memset(VP1[:, :, :, :, :], 0.0))
                pool.memset(VP1[:, :, :, :, 16:17], 1.0).then_inc(ones_pool, 1)

            for step in order("POOL"):
                kind = step[0]
                if kind in ("q", "kv"):
                    j = step[1]
                    wait_free(pool, fill[step])
                    if kind == "q":
                        parts, rem, done, n, wr = QP, QR, q_parts, P, dq_wr
                    else:
                        parts, rem, done, n, wr = KP, KR, k_parts, KV[layer(j)] * DH[layer(j)], dk_wr
                    if j >= 1:
                        pool.wait_ge(wr, 16 * j)
                    link(pool.tensor_copy(parts[0:n, 1, :], rem[0:n, :]))
                    pool.tensor_tensor(parts[0:n, 2, :], rem[0:n, :], parts[0:n, 1, :],
                                       ALU.subtract).then_inc(done, 1)
                    if step == ("kv", 1):
                        late_constants()
                elif kind == "norm":
                    _, j, p = step
                    n = 2 * j + p
                    pool.wait_ge(o_in[n % 2], 32 * (n // 2 + 1))
                    if j >= 2:
                        pool.wait_ge(fill_ready, fill[("wo", j - 2)] + 1)
                    pool.tensor_tensor(ON[:, j % 2, p, :], OP[:, j % 2, p, :], OR[:, j % 2, p, :],
                                       ALU.mult).then_inc(normed, 1)
                elif kind in ("wo", "down"):
                    b = step[1] % B
                    pool.wait_ge(mv_done, norms[step] + 1)
                    link(pool.tensor_scalar(VE[:, :], MV[:, :, 1], 1.0, EPS, ALU.mult, ALU.add))
                    link(pool.tensor_tensor(RSTD[:, :], VE[:, :], NHALF[:, :], ALU.pow))
                    for t in range(TT):
                        link(pool.tensor_scalar(NMR[:, t:t + 1], MV[:, t, 0:1], RSTD[:, t:t + 1], -1.0,
                                                ALU.mult, ALU.mult))
                    for t in range(TT):
                        ins = pool.tensor_scalar(X[:, b, t, :], X[:, b, t, :], RSTD[:, t:t + 1],
                                                 NMR[:, t:t + 1], ALU.mult, ALU.add)
                    ins.then_inc(x_new, 1)
                elif kind == "lut1":
                    _, c, part = step
                    pool.wait_ge(bit_done, c + 1)
                    for i in range(2 * part, 2 * part + 2):
                        ins = pool.tensor_scalar(LV[:, i, :], LB0[:, :], LD[:, i:i + 1],
                                                 LT[:, 2 * i:2 * i + 1], ALU.mult, ALU.add)
                    ins.then_inc(level1, 1)

        @block.scalar
        def _(act):
            for step in order("ACT"):
                kind = step[0]
                if kind in ("q", "kv", "mt", "tr", "gu"):
                    n = fill[step]
                    bank = FB[n % 2]
                    act.wait_ge(fill_ready, n + 1)
                if kind == "q":
                    j = step[1]
                    if j >= 1:
                        act.wait_ge(dq_wr, 16 * j)
                    act.activation(QP[:, 0, :], bank[:, :], ACT.Copy).then_inc(q_hi, 1)
                elif kind == "kv":
                    j = step[1]
                    l = layer(j)
                    nv = KV[l] * DH[l]
                    if j in (0, B):
                        act.wait_ge(ones_pool, 2 if j == 0 else 3)
                    if j >= NST:
                        act.wait_ge(pv_mm, 4 * (j - NST + 1))
                    for kt in range(2):
                        src = bank[:, S + kt * nv:S + (kt + 1) * nv].rearrange("p (g d) -> p g d", g=8)
                        dst = VP0[:, j % NST, kt, :, 16:24] if l == 0 else VP1[:, j % NST, kt, :, 0:16]
                        act.activation(dst, src, ACT.Copy)
                    if j >= 1:
                        act.wait_ge(dk_wr, 16 * j)
                    act.activation(KP[0:nv, 0, :], bank[0:nv, 0:S], ACT.Copy).then_inc(k_hi, 1)
                elif kind == "mt":
                    j = step[1]
                    h = HEADS[layer(j)]
                    if j >= 1:
                        act.wait_ge(m_rows, rows_count(j - 1))
                    act.activation(MP[0:h, 0, :], bank[0:h, 0:S], ACT.Copy, scale=-1.0).then_inc(m_hi, 1)
                elif kind == "tr":
                    b = step[1] % B
                    act.activation(XT[:, b, :, :].rearrange("p t s -> p (t s)"), bank[:, :],
                                   ACT.Copy).then_inc(fill_free[n % 2], 1)
                elif kind == "gu":
                    _, j, i = step
                    r = rows(layer(j), i)
                    if layer(j) == 0:
                        if i == 0:
                            act.wait_ge(scales_dve, 1)
                        scale = GSH[:, i:i + 1]
                    else:
                        scale = 0.5
                    c = 6 * j + i
                    if c >= 2:
                        before = ("gu", (c - 2) // 6, (c - 2) % 6)
                        wait_free(act, fill[before])
                    act.activation(TH[0:r, c % 2, :], bank[0:r, 0:S], ACT.Tanh,
                                   scale=scale[0:r] if layer(j) == 0 else scale).then_inc(th_done, 1)
                elif kind == "score":
                    _, j, u = step
                    unit = unit0(j) + u
                    if unit >= PB_UNITS:
                        act.wait_ge(pv_mm, region_of(unit - PB_UNITS) + 1)
                    for kt in range(2):
                        n = 2 * unit + kt
                        act.wait_ge(score_mm, n + 1)
                        act.activation(PB[:, unit % PB_UNITS, kt, :, :], SC[n % 3][:, :, :], ACT.Exp,
                                       scale=DH[layer(j)] ** -0.5).then_inc(exp_done, 1)
                elif kind == "bounce":
                    _, j, p = step
                    n = 2 * j + p
                    act.wait_ge(pv_mm, 2 * (n + 1))
                    if n >= 2:
                        act.wait_ge(do_wr, 16 * (n - 1))
                    act.activation(ST[:, n % 2, :], PV[:, :, :].rearrange("p r s -> p (r s)"),
                                   ACT.Copy).then_inc(staged, 1)
                elif kind == "q8":
                    c = step[1]
                    act.wait_ge(ld_raw, 16 * (c + 1))
                    if c >= 1:
                        act.wait_ge(q8_used, c)
                    act.activation(Q8A[:, :], RAW[:, :], ACT.Copy, saturate=False)
                    act.activation(Q8B[:, :], RAW[:, :], ACT.Copy, scale=0.25,
                                   saturate=False).then_inc(q8_cast, 1)

        @block.vector
        def _(dve):
            own = [0]

            def link(ins):
                own[0] += 1
                ins.then_inc(dve_own, 1)
                dve.wait_ge(dve_own, own[0])

            def layer_norm(b, step):
                if norms[step] >= 1:
                    dve.wait_ge(x_new, norms[step])
                for t in range(TT):
                    ins = dve.bn_stats(BST[:, t, :], X[:, b, t, :])
                link(ins)
                for t in range(TT):
                    ins = dve.bn_aggr(MV[:, t, :], BST[:, t, :])
                ins.then_inc(mv_done, 1)

            for step in order("DVE"):
                kind = step[0]
                if kind in FILL:
                    n = fill[step]
                    bank = FB[n % 2]
                if kind == "q":
                    j = step[1]
                    dve.wait_ge(q_hi, j + 1)
                    if j >= 1:
                        dve.wait_ge(q_parts, j)
                    dve.tensor_tensor(QR[:, :], bank[:, :], QP[:, 0, :],
                                      ALU.subtract).then_inc(fill_free[n % 2], 1)
                elif kind == "kv":
                    j = step[1]
                    nk = KV[layer(j)] * DH[layer(j)]
                    dve.wait_ge(k_hi, j + 1)
                    if j >= 1:
                        dve.wait_ge(k_parts, j)
                    dve.tensor_tensor(KR[0:nk, :], bank[0:nk, 0:S], KP[0:nk, 0, :],
                                      ALU.subtract).then_inc(fill_free[n % 2], 1)
                elif kind == "max":
                    _, j, u = step
                    if u == 0 and j >= 2:
                        dve.wait_ge(fill_ready, fill[("mt", j - 2)] + 1)
                    for e in range(2):
                        m = 2 * (unit0(j) + u) + e
                        if layer(j) == 0:
                            g, qt = u // 2, u % 2
                            col = 16 * (g % 2) + 4 * (g // 2) + 2 * e
                        else:
                            qt = u % 2
                            col = 4 * (u // 2) + 2 * e
                        dve.wait_ge(max_mm, m + 1)
                        dve.tensor_reduce(MX[:, j % 2, qt, col:col + 2], MM[m % 2][:, :, :],
                                          axis=AX.X, op=ALU.max).then_inc(max_red, 1)
                elif kind == "mt":
                    j = step[1]
                    h = HEADS[layer(j)]
                    dve.wait_ge(m_hi, j + 1)
                    link(dve.scalar_tensor_tensor(out=MP[0:h, 1, :], in0=bank[0:h, 0:S], scalar=-1.0,
                                                  in1=MP[0:h, 0, :], op0=ALU.mult, op1=ALU.subtract))
                    dve.sem_inc(m_parts, 1)
                    dve.sem_inc(fill_free[n % 2], 1)
                elif kind == "recip":
                    _, j, p = step
                    m = 2 * j + p
                    w = 32 if layer(j) == 0 else 16
                    dve.wait_ge(sums_in, 16 * (m + 1))
                    if m >= 2:
                        dve.wait_ge(dr_wr, 16 * (m - 1))
                    dve.reciprocal(RCP[:, m % 2, 0:w], SUMS[:, m % 2, 0:w]).then_inc(recip_done, 1)
                elif kind == "wo":
                    j = step[1]
                    b = j % B
                    dve.wait_ge(fill_ready, n + 1)
                    if j == 0:
                        dve.wait_ge(ld_s, 16 * 6)
                    x2 = X[:, b, :, :].rearrange("p t d -> p (t d)")
                    dve.tensor_tensor(x2, bank[:, :], x2, ALU.add).then_inc(fill_free[n % 2], 1)
                    wait_free(dve, n)
                    layer_norm(b, step)
                elif kind == "down":
                    j = step[1]
                    b = j % B
                    x2 = X[:, b, :, :].rearrange("p t d -> p (t d)")
                    dve.wait_ge(fill_ready, n + 1)
                    if layer(j) == 0:
                        for t in range(TT):
                            ins = dve.tensor_tensor(YD[:, t, :], bank[:, t * D:(t + 1) * D], DS[:, :], ALU.mult)
                        ins.then_inc(fill_free[n % 2], 1)
                        wait_free(dve, n)
                        link(dve.tensor_tensor(x2, YD[:, :, :].rearrange("p t d -> p (t d)"), x2, ALU.add))
                    else:
                        dve.tensor_tensor(x2, bank[:, :], x2, ALU.add).then_inc(fill_free[n % 2], 1)
                        wait_free(dve, n)
                    layer_norm(b, step)
                elif kind == "gu":
                    _, j, i = step
                    r = rows(layer(j), i)
                    dve.wait_ge(th_done, 6 * j + i + 1)
                    if i == 0 and j >= 1:
                        dve.wait_ge(fill_ready, fill[("down", j - 1)] + 1)
                    if 6 * j + i >= 1:
                        wait_free(dve, fill["gu", (6 * j + i - 1) // 6, (i + 5) % 6])
                    link(dve.scalar_tensor_tensor(out=AA[0:r, :], in0=TH[0:r, (6 * j + i) % 2, :], scalar=1.0,
                                                  in1=bank[0:r, 0:S], op0=ALU.add, op1=ALU.mult))
                    c = GUS[0:r, i:i + 1] if layer(j) == 0 else 0.5
                    dve.scalar_tensor_tensor(out=HT[0:r, i, :], in0=bank[0:r, S:2 * S], scalar=c,
                                             in1=AA[0:r, :], op0=ALU.mult,
                                             op1=ALU.mult).then_inc(fill_free[n % 2], 1)
                elif kind == "q8":
                    c = step[1]
                    if c == 0:
                        dve.wait_ge(ld_s, 16 * 6)
                        link(dve.tensor_scalar(GSH[:, :], GS[:, :], 0.5, None, ALU.mult))
                        dve.tensor_tensor(GUS[:, :], GSH[:, :], US[:, :], ALU.mult).then_inc(scales_dve, 1)
                        dve.tensor_tensor(LD[:, :], LT[:, 1:LUT:2], LT[:, 0:LUT:2], ALU.subtract)
                    w = W0[:, c * Q8_W:(c + 1) * Q8_W]
                    dve.wait_ge(q8_cast, c + 1)
                    link(dve.tensor_scalar(BIG[:, :], RAW[:, :], 1.0, None, ALU.is_ge))
                    dve.scalar_tensor_tensor(out=BIG[:, :], in0=RAW[:, :], scalar=-1.0, in1=BIG[:, :],
                                             op0=ALU.is_le, op1=ALU.add)
                    dve.tensor_copy(w, Q8A[:, :])
                    link(dve.tensor_scalar(QB[:, :], Q8B[:, :], 4.0, None, ALU.mult))
                    dve.copy_predicated(w, BIG[:, :], QB[:, :]).then_inc(q8_used, 1)
                    dve.wait_ge(q8_used, c + 1)
                elif kind == "lutbits":
                    c = step[1]
                    if c == 0:
                        dve.wait_ge(ld_idx, 16 * 4)
                    src = W1[:, c * LUT_W:(c + 1) * LUT_W]
                    for k in range(4):
                        ins = dve.tensor_scalar(LB[:, k, :], src, 1 << k, None, ALU.bitwise_and)
                        if k == 0:
                            link(ins)
                    dve.tensor_copy(LB0[:, :], LB[:, 0, :]).then_inc(bit_done, 1)
                elif kind in ("lut2", "lut3", "lut4"):
                    c, k = step[1], int(kind[3]) - 1
                    dve.wait_ge(level1, 4 * (c + 1))
                    gap = 1 << (k - 1)
                    for i in range(0, LUT // 2, 2 * gap):
                        ins = dve.copy_predicated(LV[:, i, :], LB[:, k, :], LV[:, i + gap, :])
                    link(ins)
                    if k == 3:
                        dve.tensor_copy(w1f[:, c * LUT_W:(c + 1) * LUT_W], LV[:, 0, :]).then_inc(lut_done, 1)
                        dve.wait_ge(lut_done, c + 1)

        @block.tensor
        def _(pe):
            for step in order("PE"):
                kind = step[0]
                if kind in FILL:
                    n = fill[step]
                    bank = FB[n % 2]
                    if n >= 2:
                        wait_free(pe, n - 2)
                if kind == "q":
                    j = step[1]
                    l, b = layer(j), j % B
                    if l == 0:
                        pe.wait_ge(ld_x0, 16)
                        if b >= 1:
                            pe.wait_ge(ld_x, 16 * (B - 1))
                        pe.wait_ge(ld_w0, 16 * 3)
                    else:
                        wait_free(pe, fill[("tr", j - B, 1)])
                        pe.wait_ge(ld_w1, 16 * 4)
                    for m in range(2):
                        for t in range(DT):
                            ins = pe.matmul(bank[:, m * S:(m + 1) * S], WQ[l][:, t, m * P:(m + 1) * P],
                                            XT[:, b, t, :], start=t == 0, stop=t == DT - 1)
                    ins.then_inc(fill_ready, 1)
                elif kind == "kv":
                    j = step[1]
                    l, b = layer(j), j % B
                    nv = KV[l] * DH[l]
                    for t in range(DT):
                        pe.matmul(bank[0:nv, 0:S], WK[l][:, t, :], XT[:, b, t, :],
                                  start=t == 0, stop=t == DT - 1)
                    for kt in range(2):
                        for t in range(DT):
                            ins = pe.matmul(bank[:, S + kt * nv:S + (kt + 1) * nv],
                                            XT[:, b, t, kt * P:(kt + 1) * P], WV[l][:, t, :],
                                            start=t == 0, stop=t == DT - 1)
                    ins.then_inc(fill_ready, 1)
                elif kind == "max":
                    _, j, u = step
                    if u == 0:
                        pe.wait_ge(stack_in[j % NST], stack_count(j))
                    r = STACK[layer(j)]
                    for e in range(2):
                        m = 2 * (unit0(j) + u) + e
                        if m >= 2:
                            pe.wait_ge(max_red, m - 1)
                        for i in range(2):
                            if layer(j) == 0:
                                g, qt, h = u // 2, u % 2, 2 * e + i
                            else:
                                g, qt, h = 2 * (u // 2) + e, u % 2, i
                            lo, ks, qs = stacked(j, g)
                            ins = pe.matmul(MM[m % 2][:, i, :],
                                            QS[lo:lo + r, j % NST, qs + h, qt * P:(qt + 1) * P],
                                            keys(j)[lo:lo + r, j % NST, ks, :], start=True, stop=True)
                        ins.then_inc(max_mm, 1)
                elif kind == "mt":
                    j = step[1]
                    h = HEADS[layer(j)]
                    pe.wait_ge(max_red, 2 * unit0(j + 1))
                    pe.wait_ge(const_pool, 2)
                    for qt in range(2):
                        ins = pe.transpose(bank[0:h, qt * P:(qt + 1) * P], MX[:, j % 2, qt, 0:h], IDN[:, :])
                    ins.then_inc(fill_ready, 1)
                elif kind == "score":
                    _, j, u = step
                    if u == 0:
                        pe.wait_ge(m_rows, rows_count(j))
                    r = STACK[layer(j)] + 2
                    if layer(j) == 0:
                        g, h = 4 * (u // 8) + u % 4, 2 * ((u // 4) % 2)
                    else:
                        g, h = u, 0
                    lo, ks, qs = stacked(j, g)
                    for kt in range(2):
                        n = 2 * (unit0(j) + u) + kt
                        if n >= 3:
                            pe.wait_ge(exp_done, n - 2)
                        pe.matmul(SC[n % 3][:, :, :],
                                  keys(j)[lo:lo + r, j % NST, ks, kt * P:(kt + 1) * P],
                                  QS[lo:lo + r, j % NST, qs + h:qs + h + 2, :],
                                  start=True, stop=True).then_inc(score_mm, 1)
                elif kind == "pv":
                    _, j, r = step
                    per = UNITS[layer(j)] // 4
                    first = unit0(j) + per * r
                    pe.wait_ge(exp_done, 2 * (first + per))
                    if r % 2 == 0 and j + r > 0:
                        pe.wait_ge(staged, 2 * j + r // 2)
                    if layer(j) == 0:
                        for kt in range(2):
                            for e in range(2):
                                for c in range(4):
                                    w = 16 - 16 * e
                                    ins = pe.matmul(PV[32 * c:32 * c + 32, r % 2, :],
                                                    VP0[:, j % NST, kt, 4 * (r // 2) + c, w:w + 32],
                                                    PB[:, (first + c) % PB_UNITS, kt, e, :],
                                                    start=kt + e == 0, stop=kt + e == 2)
                    else:
                        for kt in range(2):
                            for c in range(4):
                                ins = pe.matmul(PV[32 * c:32 * c + 32, r % 2, :],
                                                VP1[:, j % NST, kt, 2 * r + c // 2, :],
                                                PB[:, (first + c // 2) % PB_UNITS, kt, c % 2, :],
                                                start=kt == 0, stop=kt == 1)
                    ins.then_inc(pv_mm, 1)
                elif kind == "wo":
                    j = step[1]
                    if j == 0:
                        pe.wait_ge(ld_s, 16 * 6)
                    pe.wait_ge(normed, 2 * (j + 1))
                    for t in range(TT):
                        for p in range(2):
                            ins = pe.matmul(bank[:, t * D:(t + 1) * D], ON[:, j % 2, p, t * P:(t + 1) * P],
                                            WO[layer(j)][:, p, :], start=p == 0, stop=p == 1)
                    ins.then_inc(fill_ready, 1)
                elif kind == "tr":
                    _, j, w = step
                    pe.wait_ge(x_new, norms[("wo", "down")[w], j] + 1)
                    for d in range(DT):
                        for t in range(TT):
                            ins = pe.transpose(bank[:, d * S + t * P:d * S + (t + 1) * P],
                                               X[:, j % B, t, d * P:(d + 1) * P], IDN[:, :])
                    ins.then_inc(fill_ready, 1)
                elif kind == "gu":
                    _, j, i = step
                    l, b = layer(j), j % B
                    r = rows(l, i)
                    if i == 0:
                        wait_free(pe, fill[("tr", j, 0)])
                        if l == 0:
                            pe.wait_ge(q8_used, N_Q8)
                        else:
                            pe.wait_ge(lut_done, N_LUT)
                    for w in range(2):
                        for t in range(DT):
                            ins = pe.matmul(bank[0:r, w * S:(w + 1) * S], ffn_up(l, w, t, i),
                                            XT[:, b, t, :], start=t == 0, stop=t == DT - 1)
                    ins.then_inc(fill_ready, 1)
                elif kind == "down":
                    j = step[1]
                    l = layer(j)
                    for i in range(4, 6):
                        wait_free(pe, fill[("gu", j, i)])
                    for t in range(TT):
                        for i in range(6):
                            r = rows(l, i)
                            ins = pe.matmul(bank[:, t * D:(t + 1) * D], HT[0:r, i, t * P:(t + 1) * P],
                                            ffn_down(l, i), start=i == 0, stop=i == 5)
                    ins.then_inc(fill_ready, 1)


def build(nc, args):
    two_layer_kernel(nc, *args)


def kernel(**inputs):
    import numpy as np
    import concourse.bacc as bacc
    from concourse.bass_utils import run_bass_kernel_spmd

    a = {k: np.asarray(v) for k, v in inputs.items()}
    dh0 = D // 32
    wq0 = a["L0_attn_Wq"].reshape(D, 4, 2, 4, dh0).transpose(0, 2, 4, 1, 3).reshape(D, D)
    wk0 = a["L0_attn_Wk"].reshape(D, 4, 2, dh0).transpose(0, 2, 3, 1).reshape(D, 64)
    wo0 = a["L0_attn_Wo"].reshape(2, 4, 2, 2, dh0, D).transpose(0, 2, 1, 3, 4, 5).reshape(D, D)
    arrays = {
        "x": a["L0_attn_x"],
        "xt": a["L0_attn_x"].transpose(0, 2, 1),
        "wq0": wq0, "wk0": wk0, "wv0": a["L0_attn_Wv"], "wo0": wo0,
        "gate0": a["L0_ffn_gate_w"], "up0": a["L0_ffn_up_w"], "down0": a["L0_ffn_down_w"],
        "gs0": a["L0_ffn_gate_scale"].reshape(6, P).T, "us0": a["L0_ffn_up_scale"].reshape(6, P).T,
        "ds0": a["L0_ffn_down_scale"].reshape(1, D),
        "wq1": a["L1_attn_wq"].T.reshape(D, 16, 16).transpose(0, 2, 1).reshape(D, D),
        "wk1": a["L1_attn_wk"].T.reshape(D, 8, 16).transpose(0, 2, 1).reshape(D, P), "wv1": a["L1_attn_wv"].T,
        "wo1": a["L1_attn_wo"].T,
        "lut": a["L1_ffn_lut"].reshape(1, LUT),
        "gidx": a["L1_ffn_gate_idx"].T, "uidx": a["L1_ffn_up_idx"].T, "didx": a["L1_ffn_down_idx"].T,
    }
    nc = bacc.Bacc("TRN2", target_bir_lowering=False, num_devices=1)
    feeds, args = {}, []
    for name, v in arrays.items():
        v = np.ascontiguousarray(v)
        feeds["in_" + name] = v
        args.append(nc.dram_tensor("in_" + name, v.shape, mybir.dt.from_np(v.dtype), kind="ExternalInput").ap())
    args.append(nc.dram_tensor("out_0", (B, S, D), F32, kind="ExternalOutput").ap())
    build(nc, args)
    r = run_bass_kernel_spmd(nc, [feeds], core_ids=[0])
    return r.results[0]["out_0"]
```

```python
from contextlib import ExitStack

import concourse.bass as bass
from concourse import mybir

P = 128
F32 = mybir.dt.float32
F32R = mybir.dt.float32r
BF16 = mybir.dt.bfloat16
FP8 = mybir.dt.float8e4
I32 = mybir.dt.int32
ALU = mybir.AluOpType
ACT = mybir.ActivationFunctionType
AX = mybir.AxisListType

B, S, D = 4, 256, 256
HEADS = (32, 16)
KV = (8, 8)
I0, I1 = 768, 688
LUT = 16
EPS = 1e-5
DH = tuple(D // h for h in HEADS)
UNITS = tuple(h * 2 * S // 1024 for h in HEADS)
JOBS = 2 * B
DT = D // P
TT = S // P

Q_PART = (0, 0, 0, 1, 1, 2)
K_PART = (0, 1, 2, 0, 1, 0)
NPROD = len(Q_PART)
STACK = tuple(NPROD * d for d in DH)

PB_UNITS = 6
NSC = 2
NMM = 2
NFB = 3
NST = 3
Q8_W = 384
LUT_W = 330
W1_USED = 2 * DT * I1 + 6 * D
N_Q8 = (2 * DT * I0 + 6 * D) // Q8_W
N_LUT = -(-W1_USED // LUT_W)
W1_COLS = N_LUT * LUT_W


def layer(j):
    return j // B


def halves(j):
    return 2 if layer(j) == 0 else 1


def unit0(j):
    return sum(UNITS[layer(i)] for i in range(j))


SLOT = [42.01, 47.98, 47.98, 47.36, 37.65, 38.14, 38.33, 36.9]
AT = {
    "first": [-33.26], "score": [0.5, 0.43, 0.65, 0.28, 0.27, 0.43, 0.27, 0.46],
    "max": [0.77, 0.77, 0.77, 0.82, 0.82, 0.81, 0.75, 0.61],
    "max0": [-0.03, -0.0, 0.01, -0.11, -0.0, 0.1, 0.04, 0.01],
    "mt0": [0.59, 0.39, 0.46, 0.49, 0.5, 0.46, 0.43, 0.47],
    "mt1": [0.96, 0.79, 0.9, 0.89, 0.8, 1.01, 0.97, 0.76],
    "pv": [2.29, 1.91, 2.69, 2.85, 1.2, 2.01, 1.65, 2.56],
    "stage": [2.97, 1.12, 1.83, 2.67, 1.38, 2.21, 2.14, 2.37],
    "turn": [7.18, 6.11, 5.13, 6.11, 3.79, 5.55, 4.83, 5.59],
    "back": [7.55, 8.48, 8.68, 10.15, 7.31, 12.01, 7.56, 8.05],
    "wo": [18.16, 17.81, 17.7, 15.61, 12.5, 14.43, 11.51, 12.62],
    "tr0": [25.55, 25.91, 26.41, 23.58, 22.76, 24.72, 28.13, 21.15],
    "gu": [29.98, 28.06, 28.86, 30.26, 28.57, 31.55, 31.55, 25.38],
    "gu_each": [2.04, 2.07, 2.15, 1.82, 2.86, 2.45, 2.34, 2.52],
    "hsplit": [4.01, 2.76, 2.43, 2.49, 4.47, 4.3, 3.55, 3.88],
    "down": [46.09, 39.72, 44.81, 44.24, 46.29, 46.49, 55.67, 55.44],
    "tr1": [58.1, 56.75, 56.24, 52.9, 70.65, 58.74, 55.96, 55.41],
    "q": [59.91, 60.42, 58.85, 54.54, 57.5, 61.78, 71.74, 56.69],
    "kv": [62.35, 68.69, 59.9, 60.66, 60.63, 75.69, 65.15, 68.99],
    "q_first": [-56.92, -48.75, -7.99, 50.58], "kv_first": [-63.14, -37.84, 3.1, 45.0], "mid": [4.54],
    "mid_first": [6.81], "q8": [-24.87], "q8_each": [7.27], "q8w": [3.59], "lut": [42.08],
    "lut_each": [14.51], "lut1": [0.22], "lut1_each": [1.76], "lut2": [9.77], "lut3": [12.97],
    "lut4": [13.08], "lutlow": [13.62], "reload": [52.7], "ln": [5.58], "ln_down": [5.09],
    "load": [-65.21, -11.32, 1.07], "stack": [5.76], "stack_first": [11.68], "early": [4.94],
}
LAG = {
    "q": {"ACT": 1.62, "DVE": 3.21, "POOL": 2.86, "SP": 4.59},
    "kv": {"ACT": 2.26, "DVE": 3.0, "POOL": 3.81, "SP": 3.83},
    "max": {"DVE": 1.09},
    "mt": {"ACT": 1.02, "DVE": 1.37, "SP": -0.13},
    "score": {"ACT": 0.94},
    "wo": {"DVE": 2.74, "POOL": 3.27},
    "tr": {"ACT": -0.36, "DVE": 1.56},
    "gu": {"ACT": 0.35, "DVE": 1.13},
    "hsplit": {"POOL": -0.75},
    "down": {"DVE": 3.24, "POOL": 3.95},
    "q8": {"ACT": 0.94, "DVE": 2.72},
    "lutbits": {"DVE": 0.09, "ACT": 0.92},
    "lutlow": {"SP": 3.5, "ACT": 1.44, "POOL": -1.01},
    "stage": {"ACT": 1.13},
    "turn": {"DVE": 0.79},
    "back": {"ACT": 0.93},
}


WARM = {
    "mt1": [18, 0, 8, 11, 6, 0, 0, 0],
    "turn1": [1, 5, 0, 7, 0, 0, 3, 0],
    "wo": [1, 0, 0, 0, 2, 0, 0, 0],
    "gu": [3, 0, 2, 4, 2, 0, 0, 6],
    "down": [0, 3, 0, 0, 0, 0, 0, 0],
    "tr1": [0, 0, 0, 10, 0, 0, 17, 25],
    "q": [0, 0, 0, 0, 2, 0, 0, 0],
    "mt0": [0, 0, 3, 4, 2, 1, 1, 0],
    "back0": [12, 6, 0, 4, 8, 0, 0, 2],
    "back1": [0, 0, 1, 1, 3, 0, 0, 3],
    "tr0": [8, 3, 0, 0, 3, 0, 0, 1],
    "max": [12, 16, 0, 4, 0, 0, 0, 1],
    "turn0": [0, 0, 3, 5, 12, 0, 2, 0],
    "kv": [13, 11, 5, 0, 2, 1, 2, 0],
}


def due(name, j=0):
    v = AT[name]
    return v[j] if len(v) == JOBS else v[layer(j)] if len(v) == 2 else v[0]


def plan():
    start = [0.0]
    for j in range(JOBS):
        start.append(start[j] + SLOT[j])
    at = []
    for j in range(JOBS):
        l = layer(j)
        n, t0, t1, length = UNITS[l], start[j], start[j + 1], SLOT[j]
        before = start[j - 1] if j else due("first")
        span = t0 - before
        early = [due("early") if j == 0 else 0.0, 0.0]
        for u in range(n):
            at.append((t0 - early[2 * u // n] + length * (u + due("score", j)) / n, ("score", j, u)))
            at.append((before + span * (due("max0", j) + due("max", j) * u / n), ("max", j, u)))
        for p in range(2):
            at.append((before + due(f"mt{p}", j) * span, ("mt", j, p)))
        for r in range(4):
            at.append((t0 - early[r // 2] + length * (r + 1) / 4 + due("pv", j), ("pv", j, r)))
        for p in range(2):
            for kind in ("stage", "turn", "back"):
                at.append((t0 - early[p] + length * (p + 1) / 2 + due(kind, j), (kind, j, p)))
        at.append((t1 + due("wo", j), ("wo", j)))
        at.append((t1 + due("wo", j) + due("ln"), ("ln", j, 0)))
        at.append((t1 + due("tr0", j), ("tr", j, 0)))
        for i in range(6):
            t = t1 + due("gu", j) + due("gu_each", j) * i
            at.append((t, ("gu", j, i)))
            at.append((t + due("hsplit", j), ("hsplit", j, i)))
        at.append((t1 + due("down", j), ("down", j)))
        at.append((t1 + due("down", j) + due("ln_down"), ("ln", j, 1)))
        if l == 0:
            at.append((t1 + due("tr1", j), ("tr", j, 1)))
            at.append((t1 + due("q", j), ("q", j + B)))
            at.append((t1 + due("q", j) + due("mid"), ("qmid", j + B)))
            at.append((t1 + due("q", j) + due("stack"), ("qstack", j + B)))
            at.append((t1 + due("kv", j), ("kv", j + B)))
            at.append((t1 + due("kv", j) + due("mid"), ("kmid", j + B)))
            at.append((t1 + due("kv", j) + due("stack"), ("kstack", j + B)))
            for kind, x, t in (("q", "q", AT["q_first"][j]), ("kv", "k", AT["kv_first"][j])):
                at.append((t, (kind, j)))
                at.append((t + due("mid_first"), (x + "mid", j)))
                at.append((t + due("stack_first"), (x + "stack", j)))
        else:
            at.append((t1 + due("down", j) + 12.0, ("out", j)))
    for c in range(N_Q8):
        t = due("q8") + due("q8_each") * c
        at.append((t, ("q8", c)))
        at.append((t + due("q8w"), ("q8w", c)))
    for c in range(N_LUT):
        t = due("lut") + due("lut_each") * c
        at.append((t, ("lutbits", c)))
        for i in range(4):
            at.append((t + due("lut1") + due("lut1_each") * i, ("lut1", c, i)))
        for kind in ("lut2", "lut3", "lut4", "lutlow"):
            at.append((t + due(kind), (kind, c)))
    at.append((start[B] + due("reload"), ("reload",)))
    for i, t in enumerate(AT["load"]):
        at.append((t, ("load", i)))
    return at


def order(engine):
    at = plan()
    return [step for _, step in sorted(at, key=lambda x: x[0] + LAG.get(x[1][0], {}).get(engine, 0.0))]


def two_layer_kernel(nc, x, xt, wq0, wk0, wv0, wo0, gate0, up0, down0, gs0, us0, ds0,
                     wq1, wk1, wv1, wo1, lut, idx, out):
    steps = order("PE")
    FILL = ("q", "kv", "mt", "turn", "back", "wo", "tr", "gu", "down")
    fill = {}
    norms = {}
    trs = {}
    for step in steps:
        if step[0] in FILL:
            fill[step] = len(fill)
        if step[0] in ("wo", "down"):
            norms[step] = len(norms)
        if step[0] == "tr":
            trs[step] = len(trs)

    with ExitStack() as ctx:
        def sb(name, shape, dt=F32):
            return ctx.enter_context(nc.sbuf_tensor(name, shape, dt))

        def pb(name, shape, dt=F32):
            return ctx.enter_context(nc.psum_tensor(name, shape, dt))

        def sem(name):
            return ctx.enter_context(nc.semaphore(name))

        X = sb("X", [P, B, TT, D])
        XT = sb("XT", [P, 2, DT, S])
        PB = sb("PB", [P, PB_UNITS, 2, 2, S])
        QS = sb("QS", [P, NST, 16, S], BF16)
        KS0 = sb("KS0", [P, NST, 4, S], BF16)
        KS1 = sb("KS1", [P, NST, 8, S], BF16)
        VP0 = sb("VP0", [P, NST, 2, 8, 48])
        VP1 = sb("VP1", [P, NST, 2, 8, 32])
        QP = sb("QP", [P, 3, 2 * S], BF16)
        QR = sb("QR", [P, 2 * S])
        KP = sb("KP", [P, 3, S], BF16)
        KR = sb("KR", [P, S])
        MX = sb("MX", [P, 2, TT, 32])
        MP = sb("MP", [16, 2, 2, S], BF16)
        ST = sb("ST", [P, 2, 2 * S])
        RT = sb("RT", [P, 32])
        NT = sb("NT", [P, 2 * P])
        ON = sb("ON", [P, 2, S])
        WQ = [sb("WQ0", [P, DT, D]), sb("WQ1", [P, DT, D])]
        WK = [sb("WK0", [P, DT, 64]), sb("WK1", [P, DT, 128])]
        WV = [sb("WV0", [P, DT, 64]), sb("WV1", [P, DT, 128])]
        WO = [sb("WO0", [P, 2, D]), sb("WO1", [P, 2, D])]
        XH = sb("XH", [P, DT, S], F32R)
        XL = sb("XL", [P, DT, S], F32R)
        HF = sb("HF", [P, 2, S])
        HH = sb("HH", [P, 6, S], F32R)
        HL = sb("HL", [P, 6, S], F32R)
        TH = sb("TH", [P, 2, S])
        AA = sb("AA", [P, S])
        W0 = sb("W0", [P, N_Q8 * Q8_W], F32R)
        W1 = sb("W1", [P, W1_COLS], F32R)
        DS = sb("DS", [P, D])
        RAW = sb("RAW", [P, Q8_W])
        Q8A = sb("Q8A", [P, Q8_W], FP8)
        Q8B = sb("Q8B", [P, Q8_W], FP8)
        BIG = sb("BIG", [P, Q8_W], I32)
        QA = sb("QA", [P, Q8_W])
        QB = sb("QB", [P, Q8_W])
        IX = sb("IX", [P, 2, LUT_W], I32)
        LO = sb("LO", [P, LUT_W])
        LB = sb("LB", [P, 4, LUT_W], I32)
        LB0 = sb("LB0", [P, LUT_W])
        LV = sb("LV", [P, 8, LUT_W])
        LT = sb("LT", [P, LUT])
        LD = sb("LD", [P, LUT // 2])
        GS = sb("GS", [P, 6])
        US = sb("US", [P, 6])
        GSH = sb("GSH", [P, 6])
        GUS = sb("GUS", [P, 6])
        IDN = sb("IDN", [P, P])
        BST = sb("BST", [P, TT, 6])
        MV = sb("MV", [P, TT, 2])
        RSTD = sb("RSTD", [P, TT])
        VE = sb("VE", [P, TT])
        NHALF = sb("NHALF", [P, TT])

        SC = [pb(f"SC{i}", [P, 2, S]) for i in range(NSC)]
        MM = [pb(f"MM{i}", [P, 2, S]) for i in range(NMM)]
        PV = pb("PV", [P, 2, S])
        FB = [pb(f"FB{i}", [P, 2 * S]) for i in range(NFB)]

        dq = nc.dram_tensor("dq", (JOBS, 3, D, S), BF16, kind="Internal").ap()
        dk = nc.dram_tensor("dk", (JOBS, 3, P, S), BF16, kind="Internal").ap()
        dw = nc.dram_tensor("dw", (P, W1_COLS), F32, kind="Internal").ap()

        ld_xt = [sem(f"ld_xt{i}") for i in range(2)]
        ld_w0 = sem("ld_w0")
        ld_w1 = sem("ld_w1")
        ld_s = sem("ld_s")
        ld_x = sem("ld_x")
        ld_raw = sem("ld_raw")
        ld_idx = [sem(f"ld_idx{i}") for i in range(2)]
        idn_zero = sem("idn_zero")
        const_pool = sem("const_pool")
        ones_pool = sem("ones_pool")
        scales_dve = sem("scales_dve")
        fill_ready = sem("fill_ready")
        fill_free = [sem(f"fill_free{i}") for i in range(NFB)]
        q_hi = sem("q_hi")
        q_mid = sem("q_mid")
        k_mid = sem("k_mid")
        k_hi = sem("k_hi")
        q_parts = sem("q_parts")
        k_parts = sem("k_parts")
        dq_wr = sem("dq_wr")
        dk_wr = sem("dk_wr")
        stack_in = [sem(f"stack_in{i}") for i in range(NST)]
        max_mm = sem("max_mm")
        max_red = sem("max_red")
        m_hi = sem("m_hi")
        m_parts = sem("m_parts")
        m_rows = [sem(f"m_rows{i}") for i in range(2)]
        score_mm = sem("score_mm")
        exp_done = sem("exp_done")
        pv_mm = sem("pv_mm")
        staged = sem("staged")
        turned = sem("turned")
        level4 = sem("level4")
        normed = sem("normed")
        mv_done = sem("mv_done")
        rstd_done = sem("rstd_done")
        x_new = sem("x_new")
        th_done = sem("th_done")
        q8_cast = sem("q8_cast")
        q8_used = sem("q8_used")
        q8_done = sem("q8_done")
        x_hi = sem("x_hi")
        h_new = sem("h_new")
        h_hi = sem("h_hi")
        h_parts = sem("h_parts")
        low_done = sem("low_done")
        dw_wr = sem("dw_wr")
        low_in = sem("low_in")
        bit_done = sem("bit_done")
        bit0_done = sem("bit0_done")
        level1 = sem("level1")
        lut_done = sem("lut_done")
        out_wr = sem("out_wr")
        dve_own = sem("dve_own")
        pool_own = sem("pool_own")
        act_own = sem("act_own")

        block = ctx.enter_context(nc.Block())

        def wait_free(eng, n):
            eng.wait_ge(fill_free[n % NFB], n // NFB + 1)

        def stack_count(j):
            return 16 * sum(6 * halves(i) for i in range(j % NST, j + 1, NST))

        def rows_count(n):
            return 16 * sum(2 * halves(i // 2) for i in range(n % 2, n + 1, 2))

        def region_of(unit):
            first = unit0(B)
            return unit // 4 if unit < first else 4 * B + (unit - first) // 2

        def ffn_up(l, which, dt, i):
            o = which * DT * (I0, I1)[l] + dt * (I0, I1)[l] + i * P
            return (W0[:, o:o + P],) if l == 0 else (W1[:, o:o + P], W0[:, o:o + P])

        def ffn_down(l, i):
            o = 2 * DT * (I0, I1)[l] + i * D
            r = rows(l, i)
            return (W0[0:r, o:o + D],) if l == 0 else (W1[0:r, o:o + D], W0[0:r, o:o + D])

        def rows(l, i):
            return min(P, (I0, I1)[l] - i * P)

        def stacked(j, g):
            if layer(j) == 0:
                return 64 * (g % 2), g // 2, 4 * (g // 2)
            return 0, g, 2 * g

        def keys(j):
            return KS0 if layer(j) == 0 else KS1

        @block.sync
        def _(sp):
            def load_xt(b):
                sp.dma_start(XT[:, b % 2, :, :],
                             xt[b].rearrange("(t p) s -> p t s", p=P)).then_inc(ld_xt[b % 2], 16)

            load_xt(0)
            sp.dma_start(WQ[0][:, :, :], wq0.rearrange("(t p) n -> p t n", p=P)).then_inc(ld_w0, 16)
            sp.dma_start(WK[0][:, :, :], wk0.rearrange("(t p) n -> p t n", p=P)).then_inc(ld_w0, 16)
            sp.dma_start(WV[0][:, :, :], wv0.rearrange("(t p) n -> p t n", p=P)).then_inc(ld_w0, 16)
            raw = [gate0, up0]

            def load_raw(c):
                if c >= 1:
                    sp.wait_ge(q8_used, c)
                per = I0 // Q8_W
                if c < 2 * DT * per:
                    w, t, o = raw[c // (DT * per)], c // per % DT, c % per * Q8_W
                    sp.dma_start(RAW[:, :], w[t * P:(t + 1) * P, o:o + Q8_W]).then_inc(ld_raw, 16)
                else:
                    o = (c - 2 * DT * per) * Q8_W
                    sp.dma_start(RAW[:, :], down0[:, o:o + Q8_W]).then_inc(ld_raw, 16)

            def load_idx(c):
                sp.dma_start(IX[:, c % 2, :], idx[:, c * LUT_W:(c + 1) * LUT_W]).then_inc(ld_idx[c % 2], 16)

            for step in order("SP"):
                kind = step[0]
                if kind == "q":
                    j = step[1]
                    sp.wait_ge(q_parts, j + 1)
                    sp.dma_start(dq[j].rearrange("a (m p) s -> p a m s", p=P),
                                 QP[:, :, :].rearrange("p a (m s) -> p a m s", m=2)).then_inc(dq_wr, 16)
                elif kind == "qstack":
                    j = step[1]
                    sp.wait_ge(dq_wr, 16 * (j + 1))
                    if j >= NST:
                        sp.wait_ge(score_mm, 2 * unit0(j - NST + 1))
                    for half in range(halves(j)):
                        for i, n in ((0, 3), (3, 2), (5, 1)):
                            dh = DH[layer(j)]
                            lo = 64 * half + dh * i
                            src = dq[j, Q_PART[i]].rearrange("(f o d h) s -> f o d (h s)", f=halves(j), o=1, d=dh)
                            sp.dma_start(QS[lo:lo + dh * n, j % NST, :, :].rearrange("p h s -> p (h s)"),
                                         src[half].broadcast_to((n, dh, 16 * S))
                                         ).then_inc(stack_in[j % NST], 16)
                elif kind == "kv":
                    j = step[1]
                    dh = DH[layer(j)]
                    nk = KV[layer(j)] * dh
                    sp.wait_ge(k_parts, j + 1)
                    sp.dma_start(dk[j, :, 0:nk, :].rearrange("a p s -> p a s"),
                                 KP[0:nk, :, :]).then_inc(dk_wr, 16)
                elif kind == "kstack":
                    j = step[1]
                    dh = DH[layer(j)]
                    nk = KV[layer(j)] * dh
                    sp.wait_ge(dk_wr, 16 * (j + 1))
                    ks = keys(j)
                    if j >= NST:
                        sp.wait_ge(score_mm, 2 * unit0(j - NST + 1))
                    if j in (0, B):
                        sp.wait_ge(ones_pool, 1 if j == 0 else 3)
                    for half in range(halves(j)):
                        for i, m in ((0, 3), (3, 2), (5, 1)):
                            lo = 64 * half + dh * i
                            src = dk[j, 0:m, 0:nk, :].rearrange("a (f d h) s -> f a d (h s)", f=halves(j), d=dh)
                            sp.dma_start(ks[lo:lo + dh * m, j % NST, :, :].rearrange("p h s -> p (h s)"),
                                         src[half]).then_inc(stack_in[j % NST], 16)
                    if 2 <= j + 2 < B:
                        sp.wait_ge(fill_ready, max(fill["q", j], fill["kv", j]) + 1)
                        load_xt(j + 2)
                elif kind == "load":
                    if step[1] == 0:
                        sp.dma_start(DS[:, :], ds0.broadcast_to((P, D))).then_inc(ld_s, 16)
                        sp.dma_start(GS[:, :], gs0).then_inc(ld_s, 16)
                        sp.dma_start(US[:, :], us0).then_inc(ld_s, 16)
                        sp.dma_start(LT[:, :], lut.broadcast_to((P, LUT))).then_inc(ld_s, 16)
                        load_raw(0)
                        load_xt(1)
                    elif step[1] == 1:
                        sp.dma_start(X[:, :, :, :].rearrange("p b t d -> p (b t) d"),
                                     x.rearrange("b (t p) d -> p (b t) d", p=P)).then_inc(ld_x, 16)
                        sp.dma_start(WO[0][:, :, :], wo0.rearrange("(t p) n -> p t n", p=P)).then_inc(ld_x, 16)
                        load_idx(0)
                        load_idx(1)
                    else:
                        sp.dma_start(WQ[1][:, :, :], wq1.rearrange("(t p) n -> p t n", p=P)).then_inc(ld_w1, 16)
                        sp.dma_start(WK[1][:, :, :], wk1.rearrange("(t p) n -> p t n", p=P)).then_inc(ld_w1, 16)
                        sp.dma_start(WV[1][:, :, :], wv1.rearrange("(t p) n -> p t n", p=P)).then_inc(ld_w1, 16)
                        sp.dma_start(WO[1][:, :, :], wo1.rearrange("(t p) n -> p t n", p=P)).then_inc(ld_w1, 16)
                elif kind == "mt":
                    _, j, p = step
                    n = 2 * j + p
                    sp.wait_ge(m_parts, n + 1)
                    w = 8
                    for half in range(halves(j)):
                        for part in range(2):
                            row = 64 * half + STACK[layer(j)] + part
                            sp.dma_start(QS[row:row + 1, j % NST, w * p:w * p + w, :],
                                         MP[w * half:w * half + w, n % 2, part, :]).then_inc(m_rows[n % 2], 16)
                elif kind == "q8":
                    if step[1] + 1 < N_Q8:
                        load_raw(step[1] + 1)
                elif kind == "lutbits":
                    c = step[1]
                    if 1 <= c < N_LUT - 1:
                        sp.wait_ge(bit_done, c)
                        load_idx(c + 1)
                elif kind == "lutlow":
                    c = step[1]
                    sp.wait_ge(low_done, c + 1)
                    sp.dma_start(dw[:, c * LUT_W:(c + 1) * LUT_W], LO[:, :]).then_inc(dw_wr, 16)
                elif kind == "reload":
                    sp.wait_ge(dw_wr, 16 * N_LUT)
                    sp.wait_ge(fill_ready, fill["down", B - 1] + 1)
                    sp.dma_start(W0[:, 0:W1_COLS].bitcast(F32), dw).then_inc(low_in, 16)
                elif kind == "out":
                    j = step[1]
                    sp.wait_ge(x_new, norms[("down", j)] + 1)
                    sp.dma_start(out[j - B].rearrange("(t p) d -> p t d", p=P),
                                 X[:, j - B, :, :]).then_inc(out_wr, 16)
            sp.wait_ge(out_wr, 16 * B)

        @block.gpsimd
        def _(pool):
            own = [0]

            def link(ins):
                own[0] += 1
                ins.then_inc(pool_own, 1)
                pool.wait_ge(pool_own, own[0])

            pool.memset(IDN[:, :], 0.0).then_inc(idn_zero, 1)
            pool.wait_ge(idn_zero, 1)
            pool.affine_select(out=IDN[:, :], in_=IDN[:, :], compare_op=ALU.not_equal, fill=1.0,
                               base=0, pattern=[[-1, P]], channel_multiplier=1).then_inc(const_pool, 1)
            pool.memset(KS0[:, :, :, :], 1.0).then_inc(ones_pool, 1)
            link(pool.memset(VP0[:, :, :, :, :], 0.0))
            pool.memset(VP0[:, :, :, :, 24:25], 1.0).then_inc(ones_pool, 1)
            link(pool.memset(NHALF[:, :], -0.5))

            def late_constants():
                pool.memset(KS1[:, :, :, :], 1.0)
                link(pool.memset(VP1[:, :, :, :, :], 0.0))
                pool.memset(VP1[:, :, :, :, 16:17], 1.0).then_inc(ones_pool, 1)

            for step in order("POOL"):
                kind = step[0]
                if kind in ("q", "kv"):
                    j = step[1]
                    if kind == "q":
                        pool.wait_ge(q_mid, j + 1)
                        pool.tensor_tensor(QP[:, 2, :], QR[:, :], QP[:, 1, :], ALU.subtract).then_inc(q_parts, 1)
                    else:
                        n = KV[layer(j)] * DH[layer(j)]
                        pool.wait_ge(k_mid, j + 1)
                        pool.tensor_tensor(KP[0:n, 2, :], KR[0:n, :], KP[0:n, 1, :],
                                           ALU.subtract).then_inc(k_parts, 1)
                    if step == ("kv", 1):
                        late_constants()
                elif kind in ("wo", "down"):
                    pool.wait_ge(mv_done, norms[step] + 1)
                    link(pool.tensor_scalar(VE[:, :], MV[:, :, 1], 1.0, EPS, ALU.mult, ALU.add))
                    pool.tensor_tensor(RSTD[:, :], VE[:, :], NHALF[:, :], ALU.pow).then_inc(rstd_done, 1)
                elif kind == "hsplit":
                    _, j, i = step
                    c, r = 6 * j + i, rows(layer(j), i)
                    pool.wait_ge(h_hi, c + 1)
                    pool.tensor_tensor(HL[0:r, i, :], HF[0:r, c % 2, :], HH[0:r, i, :].bitcast(F32),
                                       ALU.subtract).then_inc(h_parts, 1)
                elif kind == "lutlow":
                    c = step[1]
                    pool.wait_ge(lut_done, c + 1)
                    if c >= 1:
                        pool.wait_ge(dw_wr, 16 * c)
                    pool.tensor_tensor(LO[:, :], LV[:, 0, :], W1[:, c * LUT_W:(c + 1) * LUT_W].bitcast(F32),
                                       ALU.subtract).then_inc(low_done, 1)
                elif kind == "lut1":
                    _, c, part = step
                    pool.wait_ge(bit0_done, c + 1)
                    if c >= 1:
                        pool.wait_ge(low_done, c)
                    for i in range(2 * part, 2 * part + 2):
                        ins = pool.tensor_scalar(LV[:, i, :], LB0[:, :], LD[:, i:i + 1],
                                                 LT[:, 2 * i:2 * i + 1], ALU.mult, ALU.add)
                    ins.then_inc(level1, 1)

        @block.scalar
        def _(act):
            for step in order("ACT"):
                kind = step[0]
                if kind in ("q", "kv", "mt", "back", "tr", "gu"):
                    n = fill[step]
                    bank = FB[n % NFB]
                    act.wait_ge(fill_ready, n + 1)
                if kind == "q":
                    j = step[1]
                    if j >= 1:
                        act.wait_ge(dq_wr, 16 * j)
                    act.activation(QP[:, 0, :], bank[:, :], ACT.Copy).then_inc(q_hi, 1)
                elif kind == "kv":
                    j = step[1]
                    l = layer(j)
                    nv = KV[l] * DH[l]
                    if j in (0, B):
                        act.wait_ge(ones_pool, 2 if j == 0 else 3)
                    if j >= NST:
                        act.wait_ge(pv_mm, 4 * (j - NST + 1))
                    for kt in range(2):
                        src = bank[:, S + kt * nv:S + (kt + 1) * nv].rearrange("p (g d) -> p g d", g=8)
                        dst = VP0[:, j % NST, kt, :, 16:24] if l == 0 else VP1[:, j % NST, kt, :, 0:16]
                        act.activation(dst, src, ACT.Copy)
                    if j >= 1:
                        act.wait_ge(dk_wr, 16 * j)
                    act.activation(KP[0:nv, 0, :], bank[0:nv, 0:S], ACT.Copy).then_inc(k_hi, 1)
                elif kind == "qmid":
                    j = step[1]
                    wait_free(act, fill["q", j])
                    act.activation(QP[:, 1, :], QR[:, :], ACT.Copy).then_inc(q_mid, 1)
                elif kind == "kmid":
                    j = step[1]
                    n = KV[layer(j)] * DH[layer(j)]
                    wait_free(act, fill["kv", j])
                    act.activation(KP[0:n, 1, :], KR[0:n, :], ACT.Copy).then_inc(k_mid, 1)
                elif kind == "mt":
                    _, j, p = step
                    m, h = 2 * j + p, HEADS[layer(j)] // 2
                    if m >= 2:
                        act.wait_ge(m_rows[m % 2], rows_count(m - 2))
                    act.activation(MP[0:h, m % 2, 0, :], bank[0:h, 0:S], ACT.Copy, scale=-1.0).then_inc(m_hi, 1)
                elif kind == "tr":
                    _, j, w = step
                    if w == 0:
                        act.activation(XH[:, :, :].rearrange("p t s -> p (t s)"), bank[:, :],
                                       ACT.Copy).then_inc(x_hi, 1)
                    else:
                        act.activation(XT[:, j % 2, :, :].rearrange("p t s -> p (t s)"), bank[:, :],
                                       ACT.Copy).then_inc(fill_free[n % NFB], 1)
                elif kind == "hsplit":
                    _, j, i = step
                    c, r = 6 * j + i, rows(layer(j), i)
                    act.wait_ge(h_new, c + 1)
                    if i == 0 and j >= 1:
                        act.wait_ge(fill_ready, fill["down", j - 1] + 1)
                    act.activation(HH[0:r, i, :], HF[0:r, c % 2, :], ACT.Copy).then_inc(h_hi, 1)
                elif kind == "gu":
                    _, j, i = step
                    r = rows(layer(j), i)
                    if layer(j) == 0:
                        if i == 0:
                            act.wait_ge(scales_dve, 1)
                        scale = GSH[:, i:i + 1]
                    else:
                        scale = 0.5
                    c = 6 * j + i
                    if c >= 2:
                        before = ("gu", (c - 2) // 6, (c - 2) % 6)
                        wait_free(act, fill[before])
                    act.activation(TH[0:r, c % 2, :], bank[0:r, 0:S], ACT.Tanh,
                                   scale=scale[0:r] if layer(j) == 0 else scale).then_inc(th_done, 1)
                elif kind == "score":
                    _, j, u = step
                    unit = unit0(j) + u
                    if unit >= PB_UNITS:
                        act.wait_ge(pv_mm, region_of(unit - PB_UNITS) + 1)
                    for kt in range(2):
                        n = 2 * unit + kt
                        act.wait_ge(score_mm, n + 1)
                        act.activation(PB[:, unit % PB_UNITS, kt, :, :], SC[n % NSC][:, :, :], ACT.Exp,
                                       scale=DH[layer(j)] ** -0.5).then_inc(exp_done, 1)
                elif kind == "back":
                    _, j, p = step
                    if j >= 1:
                        act.wait_ge(fill_ready, fill["wo", j - 1] + 1)
                    act.activation(ON[:, p, :], bank[:, 0:S], ACT.Copy).then_inc(normed, 1)
                    act.wait_ge(normed, 2 * j + p + 1)
                    act.sem_inc(fill_free[n % NFB], 1)
                elif kind == "stage":
                    _, j, p = step
                    n = 2 * j + p
                    act.wait_ge(pv_mm, 2 * (n + 1))
                    if n >= 2:
                        act.wait_ge(fill_ready, fill["turn", step[1] - 1, step[2]] + 1)
                    act.activation(ST[:, n % 2, :], PV[:, :, :].rearrange("p r s -> p (r s)"),
                                   ACT.Copy).then_inc(staged, 1)
                elif kind == "q8":
                    c = step[1]
                    act.wait_ge(ld_raw, 16 * (c + 1))
                    if c >= 1:
                        act.wait_ge(q8_used, c)
                        act.wait_ge(q8_done, c)
                    act.activation(Q8A[:, :], RAW[:, :], ACT.Copy, saturate=False)
                    act.activation(Q8B[:, :], RAW[:, :], ACT.Copy, scale=0.25, saturate=False).then_inc(act_own, 1)
                    act.wait_ge(act_own, c + 1)
                    act.activation(RAW[:, :], RAW[:, :], ACT.Abs)
                    act.activation(QA[:, :], Q8A[:, :], ACT.Copy)
                    act.activation(QB[:, :], Q8B[:, :], ACT.Copy, scale=4.0).then_inc(q8_cast, 1)
                elif kind == "lutbits":
                    act.wait_ge(bit_done, step[1] + 1)
                    if step[1] >= 1:
                        act.wait_ge(level1, 4 * step[1])
                    act.activation(LB0[:, :], LB[:, 0, :], ACT.Copy).then_inc(bit0_done, 1)
                elif kind == "lutlow":
                    c = step[1]
                    act.wait_ge(level4, c + 1)
                    act.activation(W1[:, c * LUT_W:(c + 1) * LUT_W], LV[:, 0, :], ACT.Copy).then_inc(lut_done, 1)
                elif kind == "q8w":
                    c = step[1]
                    act.wait_ge(q8_used, c + 1)
                    act.activation(W0[:, c * Q8_W:(c + 1) * Q8_W], QA[:, :], ACT.Copy).then_inc(q8_done, 1)

        @block.vector
        def _(dve):
            own = [0]

            def link(ins):
                own[0] += 1
                ins.then_inc(dve_own, 1)
                dve.wait_ge(dve_own, own[0])

            def layer_norm(b, step):
                if norms[step] >= 1:
                    dve.wait_ge(x_new, norms[step])
                for t in range(TT):
                    ins = dve.bn_stats(BST[:, t, :], X[:, b, t, :])
                link(ins)
                for t in range(TT):
                    ins = dve.bn_aggr(MV[:, t, :], BST[:, t, :])
                ins.then_inc(mv_done, 1)

            for step in order("DVE"):
                kind = step[0]
                if kind in FILL:
                    n = fill[step]
                    bank = FB[n % NFB]
                if kind == "q":
                    j = step[1]
                    dve.wait_ge(q_hi, j + 1)
                    if j >= 1:
                        dve.wait_ge(q_parts, j)
                    dve.tensor_tensor(QR[:, :], bank[:, :], QP[:, 0, :],
                                      ALU.subtract).then_inc(fill_free[n % NFB], 1)
                elif kind == "kv":
                    j = step[1]
                    nk = KV[layer(j)] * DH[layer(j)]
                    dve.wait_ge(k_hi, j + 1)
                    if j >= 1:
                        dve.wait_ge(k_parts, j)
                    dve.tensor_tensor(KR[0:nk, :], bank[0:nk, 0:S], KP[0:nk, 0, :],
                                      ALU.subtract).then_inc(fill_free[n % NFB], 1)
                elif kind == "max":
                    _, j, u = step
                    if u == 0 and j >= 2:
                        dve.wait_ge(fill_ready, fill["mt", j - 2, 1] + 1)
                    for e in range(2):
                        m = 2 * (unit0(j) + u) + e
                        if layer(j) == 0:
                            g, qt = u // 2, u % 2
                            col = 16 * (g // 4) + 8 * (g % 2) + 4 * (g // 2 % 2) + 2 * e
                        else:
                            qt = u % 2
                            col = 4 * (u // 2) + 2 * e
                        dve.wait_ge(max_mm, m + 1)
                        dve.tensor_reduce(MX[:, j % 2, qt, col:col + 2], MM[m % NMM][:, :, :],
                                          axis=AX.X, op=ALU.max).then_inc(max_red, 1)
                elif kind == "mt":
                    _, j, p = step
                    m, h = 2 * j + p, HEADS[layer(j)] // 2
                    dve.wait_ge(m_hi, m + 1)
                    link(dve.scalar_tensor_tensor(out=MP[0:h, m % 2, 1, :], in0=bank[0:h, 0:S], scalar=-1.0,
                                                  in1=MP[0:h, m % 2, 0, :], op0=ALU.mult, op1=ALU.subtract))
                    dve.sem_inc(m_parts, 1)
                    dve.sem_inc(fill_free[n % NFB], 1)
                elif kind == "turn":
                    _, j, p = step
                    m = 2 * j + p
                    w, dh = HEADS[layer(j)], DH[layer(j)]
                    dve.wait_ge(fill_ready, n + 1)
                    if m >= 1:
                        dve.wait_ge(fill_ready, fill["back", (m - 1) // 2, (m - 1) % 2] + 1)
                    heads = bank[:, :].rearrange("q (h o) -> q h o", h=w)
                    recip = RT[:, 0:w].rearrange("q (h o) -> q h o", o=1)
                    link(dve.reciprocal(recip, heads[:, :, dh:dh + 1]))
                    dve.tensor_tensor(NT[:, :].rearrange("q (h o) -> q h o", h=w), heads[:, :, 0:dh],
                                      recip.broadcast_to((P, w, dh)), ALU.mult).then_inc(turned, 1)
                    dve.wait_ge(turned, m + 1)
                    dve.sem_inc(fill_free[n % NFB], 1)
                elif kind == "wo":
                    j = step[1]
                    b = j % B
                    dve.wait_ge(fill_ready, n + 1)
                    if j == 0:
                        dve.wait_ge(ld_x, 16 * 2)
                    x2 = X[:, b, :, :].rearrange("p t d -> p (t d)")
                    dve.tensor_tensor(x2, bank[:, :], x2, ALU.add).then_inc(fill_free[n % NFB], 1)
                    wait_free(dve, n)
                    layer_norm(b, step)
                elif kind == "down":
                    j = step[1]
                    b = j % B
                    x2 = X[:, b, :, :].rearrange("p t d -> p (t d)")
                    dve.wait_ge(fill_ready, n + 1)
                    if layer(j) == 0:
                        for t in range(TT):
                            ins = dve.tensor_tensor(bank[:, t * D:(t + 1) * D], bank[:, t * D:(t + 1) * D],
                                                    DS[:, :], ALU.mult)
                        link(ins)
                    dve.tensor_tensor(x2, bank[:, :], x2, ALU.add).then_inc(fill_free[n % NFB], 1)
                    wait_free(dve, n)
                    layer_norm(b, step)
                elif kind == "ln":
                    _, j, w = step
                    dve.wait_ge(rstd_done, norms[("wo", "down")[w], j] + 1)
                    for t in range(TT):
                        ins = dve.tensor_scalar(X[:, j % B, t, :], X[:, j % B, t, :], MV[:, t, 0:1],
                                                RSTD[:, t:t + 1], ALU.subtract, ALU.mult)
                    ins.then_inc(x_new, 1)
                elif kind == "gu":
                    _, j, i = step
                    r = rows(layer(j), i)
                    dve.wait_ge(th_done, 6 * j + i + 1)
                    if 6 * j + i >= 2:
                        dve.wait_ge(h_parts, 6 * j + i - 1)
                    link(dve.scalar_tensor_tensor(out=AA[0:r, :], in0=TH[0:r, (6 * j + i) % 2, :], scalar=1.0,
                                                  in1=bank[0:r, 0:S], op0=ALU.add, op1=ALU.mult))
                    c = GUS[0:r, i:i + 1] if layer(j) == 0 else 0.5
                    link(dve.scalar_tensor_tensor(out=HF[0:r, (6 * j + i) % 2, :], in0=bank[0:r, S:2 * S],
                                                  scalar=c, in1=AA[0:r, :], op0=ALU.mult, op1=ALU.mult))
                    dve.sem_inc(h_new, 1)
                    dve.sem_inc(fill_free[n % NFB], 1)
                elif kind == "tr" and step[2] == 0:
                    dve.wait_ge(x_hi, step[1] + 1)
                    dve.tensor_tensor(XL[:, :, :].rearrange("p t s -> p (t s)"), bank[:, :],
                                      XH[:, :, :].rearrange("p t s -> p (t s)").bitcast(F32),
                                      ALU.subtract).then_inc(fill_free[n % NFB], 1)
                elif kind == "q8":
                    c = step[1]
                    if c == 0:
                        dve.wait_ge(ld_s, 16 * 4)
                        link(dve.tensor_scalar(GSH[:, :], GS[:, :], 0.5, None, ALU.mult))
                        dve.tensor_tensor(GUS[:, :], GSH[:, :], US[:, :], ALU.mult).then_inc(scales_dve, 1)
                        dve.tensor_tensor(LD[:, :], LT[:, 1:LUT:2], LT[:, 0:LUT:2], ALU.subtract)
                    dve.wait_ge(q8_cast, c + 1)
                    link(dve.tensor_scalar(BIG[:, :], RAW[:, :], 1.0, None, ALU.is_ge))
                    dve.copy_predicated(QA[:, :], BIG[:, :], QB[:, :]).then_inc(q8_used, 1)
                    dve.wait_ge(q8_used, c + 1)
                elif kind == "lutbits":
                    c = step[1]
                    dve.wait_ge(ld_idx[c % 2], 16 * (c // 2 + 1))
                    if c >= 1:
                        dve.wait_ge(bit0_done, c)
                    src = IX[:, c % 2, :]
                    for k in range(4):
                        ins = dve.tensor_scalar(LB[:, k, :], src, 1 << k, None, ALU.bitwise_and)
                    ins.then_inc(bit_done, 1)
                elif kind in ("lut2", "lut3", "lut4"):
                    c, k = step[1], int(kind[3]) - 1
                    dve.wait_ge(level1, 4 * (c + 1))
                    gap = 1 << (k - 1)
                    for i in range(0, LUT // 2, 2 * gap):
                        ins = dve.copy_predicated(LV[:, i, :], LB[:, k, :], LV[:, i + gap, :])
                    link(ins)
                    if k == 3:
                        dve.sem_inc(level4, 1)

        @block.tensor
        def _(pe):
            pe.wait_ge(const_pool, 1)

            def keep_warm(name, j, out):
                for _ in range(WARM[name][j] if name in WARM else 0):
                    pe.matmul(out, IDN[:, :], IDN[:, :], start=True, stop=True)

            for step in order("PE"):
                kind = step[0]
                if kind in FILL:
                    n = fill[step]
                    bank = FB[n % NFB]
                    if n >= NFB:
                        wait_free(pe, n - NFB)
                    name = kind + str(step[2]) if kind in ("mt", "turn", "back", "tr") else kind
                    if kind != "gu" or step[2] == 0:
                        keep_warm(name, step[1], bank[:, 0:P])
                if kind == "q":
                    j = step[1]
                    l, b = layer(j), j % 2
                    if l == 0:
                        pe.wait_ge(ld_xt[j % 2], 16 * (j // 2 + 1))
                        pe.wait_ge(ld_w0, 16 * 3)
                    else:
                        wait_free(pe, fill[("tr", j - B, 1)])
                        pe.wait_ge(ld_w1, 16 * 4)
                    for m in range(2):
                        for t in range(DT):
                            ins = pe.matmul(bank[:, m * S:(m + 1) * S], WQ[l][:, t, m * P:(m + 1) * P],
                                            XT[:, b, t, :], start=t == 0, stop=t == DT - 1)
                    ins.then_inc(fill_ready, 1)
                elif kind == "kv":
                    j = step[1]
                    l, b = layer(j), j % 2
                    nv = KV[l] * DH[l]
                    if l == 0:
                        pe.wait_ge(ld_xt[j % 2], 16 * (j // 2 + 1))
                        pe.wait_ge(ld_w0, 16 * 3)
                    else:
                        wait_free(pe, fill[("tr", j - B, 1)])
                        pe.wait_ge(ld_w1, 16 * 4)
                    for t in range(DT):
                        pe.matmul(bank[0:nv, 0:S], WK[l][:, t, :], XT[:, b, t, :],
                                  start=t == 0, stop=t == DT - 1)
                    for kt in range(2):
                        for t in range(DT):
                            ins = pe.matmul(bank[:, S + kt * nv:S + (kt + 1) * nv],
                                            XT[:, b, t, kt * P:(kt + 1) * P], WV[l][:, t, :],
                                            start=t == 0, stop=t == DT - 1)
                    ins.then_inc(fill_ready, 1)
                elif kind == "max":
                    _, j, u = step
                    if u == 0:
                        if j >= 1:
                            pe.wait_ge(max_red, 2 * unit0(j) - NMM + 1)
                        keep_warm("max", j, MM[2 * unit0(j) % NMM][:, 0, 0:P])
                        pe.wait_ge(stack_in[j % NST], stack_count(j))
                    r = STACK[layer(j)]
                    for e in range(2):
                        m = 2 * (unit0(j) + u) + e
                        if m >= NMM:
                            pe.wait_ge(max_red, m - NMM + 1)
                        for i in range(2):
                            if layer(j) == 0:
                                g, qt, h = u // 2, u % 2, 2 * e + i
                            else:
                                g, qt, h = 2 * (u // 2) + e, u % 2, i
                            lo, ks, qs = stacked(j, g)
                            ins = pe.matmul(MM[m % NMM][:, i, :],
                                            QS[lo:lo + r, j % NST, qs + h, qt * P:(qt + 1) * P],
                                            keys(j)[lo:lo + r, j % NST, ks, :], start=True, stop=True)
                        ins.then_inc(max_mm, 1)
                elif kind == "mt":
                    _, j, p = step
                    h = HEADS[layer(j)] // 2
                    pe.wait_ge(max_red, 2 * unit0(j) + UNITS[layer(j)] * (p + 1))
                    for qt in range(2):
                        ins = pe.transpose(bank[0:h, qt * P:(qt + 1) * P],
                                           MX[:, j % 2, qt, h * p:h * (p + 1)], IDN[:, :])
                    ins.then_inc(fill_ready, 1)
                elif kind == "score":
                    _, j, u = step
                    if u % (UNITS[layer(j)] // 2) == 0:
                        m = 2 * j + 2 * u // UNITS[layer(j)]
                        pe.wait_ge(m_rows[m % 2], rows_count(m))
                    r = STACK[layer(j)] + 2
                    if layer(j) == 0:
                        g, h = 4 * (u // 8) + u % 4, 2 * ((u // 4) % 2)
                    else:
                        g, h = u, 0
                    lo, ks, qs = stacked(j, g)
                    for kt in range(2):
                        n = 2 * (unit0(j) + u) + kt
                        if n >= NSC:
                            pe.wait_ge(exp_done, n - NSC + 1)
                        pe.matmul(SC[n % NSC][:, :, :],
                                  keys(j)[lo:lo + r, j % NST, ks, kt * P:(kt + 1) * P],
                                  QS[lo:lo + r, j % NST, qs + h:qs + h + 2, :],
                                  start=True, stop=True).then_inc(score_mm, 1)
                elif kind == "pv":
                    _, j, r = step
                    per = UNITS[layer(j)] // 4
                    first = unit0(j) + per * r
                    pe.wait_ge(exp_done, 2 * (first + per))
                    if r % 2 == 0 and j + r > 0:
                        pe.wait_ge(staged, 2 * j + r // 2)
                    if layer(j) == 0:
                        for kt in range(2):
                            for e in range(2):
                                for c in range(4):
                                    w = 16 - 16 * e
                                    ins = pe.matmul(PV[32 * c:32 * c + 32, r % 2, :],
                                                    VP0[:, j % NST, kt, 4 * (r // 2) + c, w:w + 32],
                                                    PB[:, (first + c) % PB_UNITS, kt, e, :],
                                                    start=kt + e == 0, stop=kt + e == 2)
                    else:
                        for kt in range(2):
                            for c in range(4):
                                ins = pe.matmul(PV[32 * c:32 * c + 32, r % 2, :],
                                                VP1[:, j % NST, kt, 2 * r + c // 2, :],
                                                PB[:, (first + c // 2) % PB_UNITS, kt, c % 2, :],
                                                start=kt == 0, stop=kt == 1)
                    ins.then_inc(pv_mm, 1)
                elif kind == "turn":
                    _, j, p = step
                    m = 2 * j + p
                    pe.wait_ge(staged, m + 1)
                    for qt in range(2):
                        for r in range(2):
                            ins = pe.transpose(bank[:, (2 * qt + r) * P:(2 * qt + r + 1) * P],
                                               ST[:, m % 2, r * S + qt * P:r * S + (qt + 1) * P], IDN[:, :])
                    ins.then_inc(fill_ready, 1)
                elif kind == "back":
                    _, j, p = step
                    pe.wait_ge(turned, 2 * j + p + 1)
                    for qt in range(2):
                        ins = pe.transpose(bank[:, qt * P:(qt + 1) * P], NT[:, qt * P:(qt + 1) * P], IDN[:, :])
                    ins.then_inc(fill_ready, 1)
                elif kind == "wo":
                    j = step[1]
                    if j == 0:
                        pe.wait_ge(ld_x, 16 * 2)
                    for p in range(2):
                        pe.wait_ge(normed, 2 * j + p + 1)
                        for t in range(TT):
                            ins = pe.matmul(bank[:, t * D:(t + 1) * D], ON[:, p, t * P:(t + 1) * P],
                                            WO[layer(j)][:, p, :], start=p + t == 0, stop=p + t == 2)
                    ins.then_inc(fill_ready, 1)
                elif kind == "tr":
                    _, j, w = step
                    pe.wait_ge(x_new, norms[("wo", "down")[w], j] + 1)
                    for d in range(DT):
                        for t in range(TT):
                            ins = pe.transpose(bank[:, d * S + t * P:d * S + (t + 1) * P],
                                               X[:, j % B, t, d * P:(d + 1) * P], IDN[:, :])
                    ins.then_inc(fill_ready, 1)
                elif kind == "gu":
                    _, j, i = step
                    l = layer(j)
                    if i == 0:
                        pe.wait_ge(x_hi, j + 1)
                        if l == 0:
                            pe.wait_ge(q8_done, N_Q8)
                        else:
                            pe.wait_ge(lut_done, N_LUT)
                            pe.wait_ge(low_in, 16)
                    for w in range(2):
                        products = [(part, xs, t) for part, xs in ((0, XH), (1, XH))[:l + 1] + ((0, XL),)
                                    for t in range(DT)]
                        for k, (part, xs, t) in enumerate(products):
                            if i == 0 and w == 0 and k == (1 + l) * DT:
                                wait_free(pe, fill["tr", j, 0])
                            ins = pe.matmul(bank[:, w * S:(w + 1) * S], ffn_up(l, w, t, i)[part], xs[:, t, :],
                                            start=k == 0, stop=k == len(products) - 1)
                    ins.then_inc(fill_ready, 1)
                elif kind == "down":
                    j = step[1]
                    l = layer(j)
                    for i in range(6):
                        pe.wait_ge(h_parts, 6 * j + i + 1)
                        products = ((0, HH), (0, HL), (1, HH))[:2 + l]
                        for k, (part, hs) in enumerate(products):
                            for t in range(TT):
                                ins = pe.matmul(bank[:, t * D:(t + 1) * D],
                                                hs[0:rows(l, i), i, t * P:(t + 1) * P], ffn_down(l, i)[part],
                                                start=i + k + t == 0,
                                                stop=(i, k, t) == (5, len(products) - 1, TT - 1))
                    ins.then_inc(fill_ready, 1)


def build(nc, args):
    two_layer_kernel(nc, *args)


def kernel(**inputs):
    import numpy as np
    import concourse.bacc as bacc
    from concourse.bass_utils import run_bass_kernel_spmd

    a = {k: np.asarray(v) for k, v in inputs.items()}
    dh0 = D // 32
    wq0 = a["L0_attn_Wq"].reshape(D, 4, 2, 4, dh0).transpose(0, 2, 4, 1, 3).reshape(D, D)
    wk0 = a["L0_attn_Wk"].reshape(D, 4, 2, dh0).transpose(0, 2, 3, 1).reshape(D, 64)
    wo0 = a["L0_attn_Wo"].reshape(2, 4, 2, 2, dh0, D).transpose(0, 2, 1, 3, 4, 5).reshape(D, D)

    def by_tile(w):
        w = np.concatenate([w, np.zeros((-len(w) % P, w.shape[1]), w.dtype)])
        return w.reshape(-1, P, w.shape[1]).transpose(1, 0, 2).reshape(P, -1)

    idx = np.concatenate([by_tile(a["L1_ffn_gate_idx"].T), by_tile(a["L1_ffn_up_idx"].T),
                          by_tile(a["L1_ffn_down_idx"].T),
                          np.zeros((P, W1_COLS - W1_USED), a["L1_ffn_gate_idx"].dtype)], axis=1)
    arrays = {
        "x": a["L0_attn_x"],
        "xt": a["L0_attn_x"].transpose(0, 2, 1),
        "wq0": wq0, "wk0": wk0, "wv0": a["L0_attn_Wv"], "wo0": wo0,
        "gate0": a["L0_ffn_gate_w"], "up0": a["L0_ffn_up_w"], "down0": by_tile(a["L0_ffn_down_w"]),
        "gs0": a["L0_ffn_gate_scale"].reshape(6, P).T, "us0": a["L0_ffn_up_scale"].reshape(6, P).T,
        "ds0": a["L0_ffn_down_scale"].reshape(1, D),
        "wq1": a["L1_attn_wq"].T.reshape(D, 16, 16).transpose(0, 2, 1).reshape(D, D),
        "wk1": a["L1_attn_wk"].T.reshape(D, 8, 16).transpose(0, 2, 1).reshape(D, P), "wv1": a["L1_attn_wv"].T,
        "wo1": a["L1_attn_wo"].T,
        "lut": a["L1_ffn_lut"].reshape(1, LUT),
        "idx": idx,
    }
    nc = bacc.Bacc("TRN2", target_bir_lowering=False, num_devices=1)
    feeds, args = {}, []
    for name, v in arrays.items():
        v = np.ascontiguousarray(v)
        feeds["in_" + name] = v
        args.append(nc.dram_tensor("in_" + name, v.shape, mybir.dt.from_np(v.dtype), kind="ExternalInput").ap())
    args.append(nc.dram_tensor("out_0", (B, S, D), F32, kind="ExternalOutput").ap())
    build(nc, args)
    r = run_bass_kernel_spmd(nc, [feeds], core_ids=[0])
    return r.results[0]["out_0"]
```
